# Optimizing a Trainium2 kernel written in Bass

```python
import numpy as np
import jax
import jax.numpy as jnp

def _softmax(x, axis=-1):
    return jax.nn.softmax(x, axis=axis)

def _gelu(x):
    return jax.nn.gelu(x, approximate=True)

def _silu(x):
    return jax.nn.silu(x)

def _sigmoid(x):
    return jax.nn.sigmoid(x)

def _layernorm(x, axis=-1, eps=1e-05):
    m = jnp.mean(x, axis=axis, keepdims=True)
    v = jnp.var(x, axis=axis, keepdims=True)
    return (x - m) / jnp.sqrt(v + eps)

def _scatter_add(tgt, idx, src, axis=0):
    return tgt.at[idx].add(src)

def _segment_sum(src, seg, n):
    return jax.ops.segment_sum(src, seg, n)
kernel_name = 'mk_cond_resid_d4_seqx_r4_5d671f'

def setup_inputs(seed: int=0):
    np.random.seed(seed)
    _w = jnp.asarray

    def _rec_inputs():
        import jax
        import jax.numpy as jnp
        _rk = jax.random.key(seed)
        x = -0.000125 + 0.9999 * jax.random.normal(jax.random.fold_in(_rk, 1), (128, 64, 1024), jnp.float32)
        _lenS = 64 - jax.random.randint(jax.random.fold_in(_rk, 7), (128,), 0, max(1, 64 // 4) + 1, jnp.int32)
        _lenS2 = 64 - jax.random.randint(jax.random.fold_in(_rk, 8), (128,), 0, max(1, 64 // 4) + 1, jnp.int32)
        cond_128 = 0.0061147 + 1.02565 * jax.random.normal(jax.random.fold_in(_rk, 11), (128, 128), jnp.float32)
        fside_S_0 = -0.022604 + 0.987366 * jax.random.normal(jax.random.fold_in(_rk, 12), (64,), jnp.float32)
        return (x, cond_128, fside_S_0)
    x, cond_128, fside_S_0 = _rec_inputs()

    def _L0_cond_setup():
        import jax, jax.numpy as jnp
        import numpy as np
        from jax import lax
        N, C_IN, L = (32, 64, 1024)
        C_OUT, K, GROUPS = (64, 9, 4)
        C_DIM, PAD, STRIDE = (128, 4, 1)
        key = jax.random.key(seed)
        k1, k2, k3, k4, k5 = jax.random.split(key, 5)
        x = jax.random.normal(k1, (N, C_IN, L), dtype=jnp.float32)
        c = jax.random.normal(k2, (N, C_DIM), dtype=jnp.float32)
        weight = jax.random.normal(k3, (C_OUT, C_IN // GROUPS, K), dtype=jnp.float32)
        c_weight = jax.random.normal(k4, (C_OUT, C_DIM), dtype=jnp.float32)
        bias = jax.random.normal(k5, (C_OUT,), dtype=jnp.float32)
        return {'x': x, 'c': c, 'weight': weight, 'c_weight': c_weight, 'bias': bias}
    _L0_cond_all = _L0_cond_setup()
    _L0_cond_in = {k: v for k, v in _L0_cond_all.items() if k in ('weight', 'c_weight')}
    del _L0_cond_all

    def _L1_cond_setup():
        import jax, jax.numpy as jnp
        import numpy as np
        K = 8
        T = 1.0
        D_EMBD = 128
        IN_C = 64
        OUT_C = 64
        BS = 32
        H = 1024
        HID = 128
        key = jax.random.key(seed)
        ks = jax.random.split(key, 10)
        s = lambda fan_in: 1.0 / np.sqrt(fan_in)
        return {'x': jax.random.normal(ks[0], (BS, IN_C, H), dtype=jnp.float32), 'embedding': jax.random.normal(ks[1], (BS, D_EMBD), dtype=jnp.float32), 'W0': jax.random.normal(ks[2], (D_EMBD, HID), dtype=jnp.float32) * s(D_EMBD), 'b0': jnp.zeros((HID,), dtype=jnp.float32), 'W1': jax.random.normal(ks[3], (HID, HID), dtype=jnp.float32) * s(HID), 'b1': jnp.zeros((HID,), dtype=jnp.float32), 'W2': jax.random.normal(ks[4], (HID, K), dtype=jnp.float32) * s(HID), 'b2': jnp.zeros((K,), dtype=jnp.float32), 'weight': jax.random.normal(ks[5], (K, OUT_C, IN_C, 1), dtype=jnp.float32) * s(IN_C), 'bias_k': jax.random.normal(ks[6], (K, OUT_C), dtype=jnp.float32) * 0.1}
    _L1_cond_all = _L1_cond_setup()
    _L1_cond_in = {k: v for k, v in _L1_cond_all.items() if k in ('W0', 'b0', 'W1', 'b1', 'W2', 'b2', 'weight', 'bias_k')}
    del _L1_cond_all

    def _L2_cond_setup():
        import jax, jax.numpy as jnp
        import numpy as np
        K = 8
        T = 1.0
        D_EMBD = 128
        IN_C = 64
        OUT_C = 64
        BS = 32
        H = 1024
        HID = 128
        key = jax.random.key(seed)
        ks = jax.random.split(key, 10)
        s = lambda fan_in: 1.0 / np.sqrt(fan_in)
        return {'x': jax.random.normal(ks[0], (BS, IN_C, H), dtype=jnp.float32), 'embedding': jax.random.normal(ks[1], (BS, D_EMBD), dtype=jnp.float32), 'W0': jax.random.normal(ks[2], (D_EMBD, HID), dtype=jnp.float32) * s(D_EMBD), 'b0': jnp.zeros((HID,), dtype=jnp.float32), 'W1': jax.random.normal(ks[3], (HID, HID), dtype=jnp.float32) * s(HID), 'b1': jnp.zeros((HID,), dtype=jnp.float32), 'W2': jax.random.normal(ks[4], (HID, K), dtype=jnp.float32) * s(HID), 'b2': jnp.zeros((K,), dtype=jnp.float32), 'weight': jax.random.normal(ks[5], (K, OUT_C, IN_C, 1), dtype=jnp.float32) * s(IN_C), 'bias_k': jax.random.normal(ks[6], (K, OUT_C), dtype=jnp.float32) * 0.1}
    _L2_cond_all = _L2_cond_setup()
    _L2_cond_in = {k: v for k, v in _L2_cond_all.items() if k in ('W0', 'b0', 'W1', 'b1', 'W2', 'b2', 'weight', 'bias_k')}
    del _L2_cond_all

    def _L3_cond_setup():
        import jax, jax.numpy as jnp
        import numpy as np
        K = 8
        T = 1.0
        D_EMBD = 128
        IN_C = 64
        OUT_C = 64
        BS = 32
        H = 1024
        HID = 128
        key = jax.random.key(seed)
        ks = jax.random.split(key, 10)
        s = lambda fan_in: 1.0 / np.sqrt(fan_in)
        return {'x': jax.random.normal(ks[0], (BS, IN_C, H), dtype=jnp.float32), 'embedding': jax.random.normal(ks[1], (BS, D_EMBD), dtype=jnp.float32), 'W0': jax.random.normal(ks[2], (D_EMBD, HID), dtype=jnp.float32) * s(D_EMBD), 'b0': jnp.zeros((HID,), dtype=jnp.float32), 'W1': jax.random.normal(ks[3], (HID, HID), dtype=jnp.float32) * s(HID), 'b1': jnp.zeros((HID,), dtype=jnp.float32), 'W2': jax.random.normal(ks[4], (HID, K), dtype=jnp.float32) * s(HID), 'b2': jnp.zeros((K,), dtype=jnp.float32), 'weight': jax.random.normal(ks[5], (K, OUT_C, IN_C, 1), dtype=jnp.float32) * s(IN_C), 'bias_k': jax.random.normal(ks[6], (K, OUT_C), dtype=jnp.float32) * 0.1}
    _L3_cond_all = _L3_cond_setup()
    _L3_cond_in = {k: v for k, v in _L3_cond_all.items() if k in ('W0', 'b0', 'W1', 'b1', 'W2', 'b2', 'weight', 'bias_k')}
    del _L3_cond_all
    return {'x': x, 'cond_128': cond_128, 'fside_S_0': fside_S_0, 'L0_cond_weight': _L0_cond_in['weight'], 'L0_cond_c_weight': _L0_cond_in['c_weight'], 'L1_cond_W0': _L1_cond_in['W0'], 'L1_cond_b0': _L1_cond_in['b0'], 'L1_cond_W1': _L1_cond_in['W1'], 'L1_cond_b1': _L1_cond_in['b1'], 'L1_cond_W2': _L1_cond_in['W2'], 'L1_cond_b2': _L1_cond_in['b2'], 'L1_cond_weight': _L1_cond_in['weight'], 'L1_cond_bias_k': _L1_cond_in['bias_k'], 'L2_cond_W0': _L2_cond_in['W0'], 'L2_cond_b0': _L2_cond_in['b0'], 'L2_cond_W1': _L2_cond_in['W1'], 'L2_cond_b1': _L2_cond_in['b1'], 'L2_cond_W2': _L2_cond_in['W2'], 'L2_cond_b2': _L2_cond_in['b2'], 'L2_cond_weight': _L2_cond_in['weight'], 'L2_cond_bias_k': _L2_cond_in['bias_k'], 'L3_cond_W0': _L3_cond_in['W0'], 'L3_cond_b0': _L3_cond_in['b0'], 'L3_cond_W1': _L3_cond_in['W1'], 'L3_cond_b1': _L3_cond_in['b1'], 'L3_cond_W2': _L3_cond_in['W2'], 'L3_cond_b2': _L3_cond_in['b2'], 'L3_cond_weight': _L3_cond_in['weight'], 'L3_cond_bias_k': _L3_cond_in['bias_k']}

def reference(x, cond_128, fside_S_0, L0_cond_weight, L0_cond_c_weight, L1_cond_W0, L1_cond_b0, L1_cond_W1, L1_cond_b1, L1_cond_W2, L1_cond_b2, L1_cond_weight, L1_cond_bias_k, L2_cond_W0, L2_cond_b0, L2_cond_W1, L2_cond_b1, L2_cond_W2, L2_cond_b2, L2_cond_weight, L2_cond_bias_k, L3_cond_W0, L3_cond_b0, L3_cond_W1, L3_cond_b1, L3_cond_W2, L3_cond_b2, L3_cond_weight, L3_cond_bias_k):
    import jax
    import jax.numpy as jnp

    def _L0_cond_ref(x, c, weight, c_weight, bias):
        import jax, jax.numpy as jnp
        import numpy as np
        from jax import lax
        N, C_IN, L = (32, 64, 1024)
        C_OUT, K, GROUPS = (64, 9, 4)
        C_DIM, PAD, STRIDE = (128, 4, 1)
        out = lax.conv_general_dilated(x, weight, window_strides=(STRIDE,), padding=[(PAD, PAD)], dimension_numbers=('NCH', 'OIH', 'NCH'), feature_group_count=GROUPS)
        ctx = jnp.einsum('nd,od->no', c, c_weight)
        out = out + ctx[:, :, None] + bias[None, :, None]
        return out

    def _L1_cond_ref(x, embedding, W0, b0, W1, b1, W2, b2, weight, bias_k):
        import jax, jax.numpy as jnp
        import numpy as np
        K = 8
        T = 1.0
        D_EMBD = 128
        IN_C = 64
        OUT_C = 64
        BS = 32
        H = 1024
        HID = 128
        h = jax.nn.gelu(embedding @ W0 + b0, approximate=False)
        h = jax.nn.gelu(h @ W1 + b1, approximate=False)
        att = jax.nn.softmax((h @ W2 + b2) / T, axis=-1)
        agg_w = jnp.einsum('bk,koi->boi', att, weight[..., 0])
        agg_b = att @ bias_k
        out = jnp.einsum('boi,bih->boh', agg_w, x) + agg_b[:, :, None]
        return out

    def _L2_cond_ref(x, embedding, W0, b0, W1, b1, W2, b2, weight, bias_k):
        import jax, jax.numpy as jnp
        import numpy as np
        K = 8
        T = 1.0
        D_EMBD = 128
        IN_C = 64
        OUT_C = 64
        BS = 32
        H = 1024
        HID = 128
        h = jax.nn.gelu(embedding @ W0 + b0, approximate=False)
        h = jax.nn.gelu(h @ W1 + b1, approximate=False)
        att = jax.nn.softmax((h @ W2 + b2) / T, axis=-1)
        agg_w = jnp.einsum('bk,koi->boi', att, weight[..., 0])
        agg_b = att @ bias_k
        out = jnp.einsum('boi,bih->boh', agg_w, x) + agg_b[:, :, None]
        return out

    def _L3_cond_ref(x, embedding, W0, b0, W1, b1, W2, b2, weight, bias_k):
        import jax, jax.numpy as jnp
        import numpy as np
        K = 8
        T = 1.0
        D_EMBD = 128
        IN_C = 64
        OUT_C = 64
        BS = 32
        H = 1024
        HID = 128
        h = jax.nn.gelu(embedding @ W0 + b0, approximate=False)
        h = jax.nn.gelu(h @ W1 + b1, approximate=False)
        att = jax.nn.softmax((h @ W2 + b2) / T, axis=-1)
        agg_w = jnp.einsum('bk,koi->boi', att, weight[..., 0])
        agg_b = att @ bias_k
        out = jnp.einsum('boi,bih->boh', agg_w, x) + agg_b[:, :, None]
        return out
    x = x + _L0_cond_ref(x, cond_128, L0_cond_weight, L0_cond_c_weight, fside_S_0)
    x = x + _L1_cond_ref(x, cond_128, L1_cond_W0, L1_cond_b0, L1_cond_W1, L1_cond_b1, L1_cond_W2, L1_cond_b2, L1_cond_weight, L1_cond_bias_k)
    x = x + _L2_cond_ref(x, cond_128, L2_cond_W0, L2_cond_b0, L2_cond_W1, L2_cond_b1, L2_cond_W2, L2_cond_b2, L2_cond_weight, L2_cond_bias_k)
    x = x + _L3_cond_ref(x, cond_128, L3_cond_W0, L3_cond_b0, L3_cond_W1, L3_cond_b1, L3_cond_W2, L3_cond_b2, L3_cond_weight, L3_cond_bias_k)
    return x

_drawn_inputs = setup_inputs


def setup_inputs(seed=0):
    import zlib

    import numpy as np

    out = dict(_drawn_inputs(seed))
    spreads = {'L1_cond_b0': (0.0, 0.705),
     'L1_cond_b1': (0.0, 0.497),
     'L1_cond_b2': (0.0, 0.397),
     'L2_cond_b0': (0.0, 0.752),
     'L2_cond_b1': (0.0, 0.412),
     'L2_cond_b2': (0.0, 0.511),
     'L3_cond_b0': (0.0, 0.622),
     'L3_cond_b1': (0.0, 0.424),
     'L3_cond_b2': (0.0, 0.319)}
    factors = {'L1_cond_bias_k': 33.013, 'L2_cond_bias_k': 33.839, 'L3_cond_bias_k': 38.737}
    for name, (base, spread) in spreads.items():
        noise = np.random.default_rng([zlib.crc32(name.encode()), seed]).standard_normal(out[name].shape)
        drawn = base * np.exp(spread * noise) if base else spread * noise
        out[name] = jnp.asarray(drawn.astype(out[name].dtype))
    for name, factor in factors.items():
        out[name] = (out[name] * factor).astype(out[name].dtype)
    return out
```

```python
from contextlib import ExitStack

import numpy as np

import concourse.bass as bass
from concourse import mybir

F32 = mybir.dt.float32
F32R = mybir.dt.float32r
ALU = mybir.AluOpType
ACT = mybir.ActivationFunctionType
AX_X = mybir.AxisListType.X

B, C, L = 128, 64, 1024
G, CG = 4, 16
TAPS, PAD = 9, 4
PH = 8
J = L // PH
QP = PH // 2
S = 4
NQ = B // S
PR = S // 2
D = 128
K = 8
KP = 32
NL = 3
N = S * J
NH = C // 2
NG = 4
TG = NH // NG


def cond_resid_kernel(nc, x_h, toep_h, eye_tap_h, cond_t, w0_h, w1_h, w2_h, b01_h, b2_h, cw_h,
                      fs_col, fs_row, mixrow_h, biask_h, mixtab_h, ident_h, parity_h, out_h):
    with ExitStack() as ctx:
        def sb(name, shape, dt=F32):
            return ctx.enter_context(nc.sbuf_tensor(name, shape, dt))

        def sem(name):
            return ctx.enter_context(nc.semaphore(name))

        bank = [ctx.enter_context(nc.psum_tensor(f"bank{i}", [128, 512], F32)) for i in range(8)]
        conv_ps, mix_ps = bank[0:4], bank[4:6]
        pair_ps, comp_ps = bank[6], bank[7]

        toep = sb("toep", [128, 2, G, QP, 32])
        eye_tap = sb("eye_tap", [128, QP * 32])
        cond = sb("cond", [128, B])
        w0 = sb("w0", [D, NL, D])
        w1 = sb("w1", [D, NL, D])
        w2 = sb("w2", [D, NL, K])
        b01 = sb("b01", [D, 2, NL])
        b2 = sb("b2", [1, NL * K])
        cw = sb("cw", [D, C])
        fcol = sb("fcol", [C, 1])
        frow = sb("frow", [1, C])
        mixrow = sb("mixrow", [C, NL, K * C])
        biask = sb("biask", [1, NL, K * C])
        mixtab = sb("mixtab", [KP, NL, NH, 2 * C])
        ident = sb("ident", [128, 128])
        parity = sb("parity", [128, 2])
        ones = sb("ones", [1, B])
        hid1 = sb("hid1", [D, NL, B])
        hid2 = sb("hid2", [D, NL, B])
        top = sb("top", [B, NL])
        expo = sb("expo", [B, NL, K])
        total = sb("total", [B, NL])
        recip = sb("recip", [B, NL])
        att = sb("att", [B, NL, K])
        att_t = sb("att_t", [KP, NL, B])
        vrow = sb("vrow", [B, C])
        vcol = sb("vcol", [C, B])
        vdup = sb("vdup", [B, G, 2, CG])
        beta = sb("beta", [128, B])
        table = [sb(f"table{n}", [128, B // 2, C]) for n in range(NL)]

        x_sb = sb("x_sb", [128, 2, G, S, J])
        y_hi = sb("y_hi", [128, 2, QP, S, J], F32R)
        y_lo = sb("y_lo", [128, 2, QP, S, J], F32R)
        out_sb = sb("out_sb", [128, 2, S, QP * J])
        a1_pair = sb("a1_pair", [128, 2, PR, C])
        a2_diag = sb("a2_diag", [128, 2, PR, 2 * C])
        a3_diag = sb("a3_diag", [128, 2, PR, 2 * C])
        a21_dup = sb("a21_dup", [128, 2, PR, G, 2, CG])
        mix_f = sb("mix_f", [128, S * G, 2, CG])
        mix_hi = sb("mix_hi", [128, 2, S, 128], F32R)
        mix_lo = sb("mix_lo", [128, 2, S, 128], F32R)

        net_in, toep_in, tab_in = sem("net_in"), sem("toep_in"), sem("tab_in")
        x_in = [sem("x_in0"), sem("x_in1")]
        stored = [sem("stored0"), sem("stored1")]
        ones_set, toep_set, zeros_set, att_ones = sem("ones_set"), sem("toep_set"), sem("zeros_set"), sem("att_ones")
        hid1_ps, hid1_set, hid2_ps, hid2_set = sem("hid1_ps"), sem("hid1_set"), sem("hid2_ps"), sem("hid2_set")
        c0_ps, c0_set = sem("c0_ps"), sem("c0_set")
        logit_ps, centred, exp_set, att_set = sem("logit_ps"), sem("centred"), sem("exp_set"), sem("att_set")
        softmax_chain, bias_chain = sem("softmax_chain"), sem("bias_chain")
        att_t_ps, att_t_set = sem("att_t_ps"), sem("att_t_set")
        prod_ps, vrow_set, vcol_ps, vcol_set = sem("prod_ps"), sem("vrow_set"), sem("vcol_ps"), sem("vcol_set")
        tab_ps, tab_act, tab_dve = sem("tab_ps"), sem("tab_act"), sem("tab_dve")
        conv_done, hi_done, lo_done = sem("conv_done"), sem("hi_done"), sem("lo_done")
        pair_in, a21_ps, a21_set, comp_done = sem("pair_in"), sem("a21_ps"), sem("a21_set"), sem("comp_done")
        mixf_set, mixhi_set, mixlo_set = sem("mixf_set"), sem("mixhi_set"), sem("mixlo_set")
        mix_done, out_act, out_dve = sem("mix_done"), sem("out_act"), sem("out_dve")

        net_loads = [(cond, cond_t), (w0, w0_h), (b01, b01_h), (cw, cw_h), (fcol, fs_col), (frow, fs_row),
                     (w1, w1_h), (w2, w2_h), (b2, b2_h), (ident, ident_h), (parity, parity_h)]
        toep_loads = [(toep, toep_h), (eye_tap, eye_tap_h)]
        tab_loads = [(mixrow, mixrow_h), (biask, biask_h), (mixtab, mixtab_h)]

        PEEL = 4

        def steps(eng, step):
            for q in range(PEEL):
                step(q, q // 2, q % 2)
            with eng.Fori(PEEL // 2, NQ // 2) as it:
                for par in range(2):
                    step(2 * it + par, it, par)

        def wait(eng, s, value):
            if not isinstance(value, int) or value > 0:
                eng.wait_ge(s, value)

        block = ctx.enter_context(nc.Block())

        @block.sync
        def _(sp):
            def load(q, par):
                sp.dma_start(x_sb[:, par].rearrange("p g s j -> p (g s j)"),
                             x_h[bass.ds(q * 128, 128), :]).then_inc(x_in[par], 16)

            def store(q, par):
                sp.wait_ge(out_act, 2 * q + 2)
                sp.wait_ge(out_dve, 2 * q + 2)
                sp.dma_start(out_h[bass.ds(q * 128, 128), :],
                             out_sb[:, par].rearrange("p s n -> p (s n)")).then_inc(stored[par], 16)

            for dst, src in net_loads:
                sp.dma_start(dst[:], src).then_inc(net_in, 16)
            for dst, src in toep_loads:
                sp.dma_start(dst[:], src).then_inc(toep_in, 16)
            load(0, 0)
            for dst, src in tab_loads:
                sp.dma_start(dst[:], src).then_inc(tab_in, 16)
            load(1, 1)

            def step(q, it, par):
                sp.wait_ge(conv_done, 4 * q + 4)
                load(q + 2, par)
                if not isinstance(q, int) or q > 0:
                    store(q - 1, 1 - par)

            for q in range(PEEL):
                step(q, q // 2, q % 2)
            with sp.Fori(PEEL // 2, NQ // 2 - 1) as it:
                for par in range(2):
                    step(2 * it + par, it, par)
            for q in range(NQ - 3, NQ):
                store(q, q % 2)
            for par in range(2):
                sp.wait_ge(stored[par], 16 * (NQ // 2))

        @block.gpsimd
        def _(pool):
            nc.gpsimd.memset(ones[:], 1.0).then_inc(ones_set, 1)
            nc.gpsimd.memset(att_t[:], 1.0).then_inc(att_ones, 1)
            nc.gpsimd.memset(a2_diag[:], 0.0).then_inc(zeros_set, 1)
            nc.gpsimd.memset(a3_diag[:], 0.0).then_inc(zeros_set, 1)
            pool.wait_ge(zeros_set, 2)
            pool.wait_ge(tab_act, 2 * TG * NL)
            pool.wait_ge(tab_dve, 2 * TG * NL)

            def step(q, it, par):
                wait(pool, a21_ps, q - 1)
                wait(pool, comp_done, q - 1)
                here = bass.ds(PR * q, PR)
                wait(pool, pair_in, 5 * q)
                n = 0
                nc.gpsimd.tensor_copy(a1_pair[:, par], table[0][:, here, :]).then_inc(pair_in, 1)
                for t, diag in ((table[1], a2_diag), (table[2], a3_diag)):
                    for h in range(2):
                        rows = slice(C * h, C * h + C)
                        pool.wait_ge(pair_in, 5 * q + n + 1)
                        n += 1
                        nc.gpsimd.tensor_copy(diag[rows, par, :, C * h:C * h + C],
                                              t[rows, here, :]).then_inc(pair_in, 1)

            steps(pool, step)

        @block.tensor
        def _(pe):
            mm = nc.tensor.matmul

            def conv(q, it, par, qp):
                if qp == 0:
                    pe.wait_ge(x_in[par], 16 * it + 16)
                wait(pe, hi_done, 4 * q + qp - 3)
                wait(pe, lo_done, 4 * q + qp - 3)
                o = conv_ps[qp][:, :].rearrange("p (s j) -> p s j", s=S)
                src, dst = (slice(0, J - 1), slice(1, J)) if qp < QP // 2 else (slice(1, J), slice(0, J - 1))
                for g in range(G):
                    mm(o[32 * g:32 * g + 32], toep[:, 0, g, qp, :], x_sb[:, par, g], start=True, stop=False)
                for g in range(G):
                    last = mm(o[32 * g:32 * g + 32, :, dst], toep[:, 1, g, qp, :], x_sb[:, par, g, :, src],
                              start=False, stop=True)
                last.then_inc(conv_done, 1)

            def compose_lower(q, par):
                pe.wait_ge(pair_in, 5 * q + 5)
                wait(pe, a21_set, 2 * q)
                for pr in range(PR):
                    last = mm(pair_ps[:, C * pr:C * pr + C], a2_diag[:, par, pr, :], a1_pair[:, par, pr, :],
                              start=True, stop=True)
                last.then_inc(a21_ps, 1)

            def compose_upper(q, par):
                pe.wait_ge(a21_set, 2 * q + 2)
                wait(pe, mixf_set, 2 * q)
                for pr in range(PR):
                    last = mm(comp_ps[:, 128 * pr:128 * pr + 128],
                              a21_dup[:, par, pr].rearrange("p g r i -> p (g r i)"), a3_diag[:, par, pr, :],
                              start=True, stop=True)
                last.then_inc(comp_done, 1)

            def mix(q, par, s):
                if s == 0:
                    pe.wait_ge(hi_done, 4 * q + 4)
                    pe.wait_ge(lo_done, 4 * q + 4)
                    pe.wait_ge(mixlo_set, q + 1)
                wait(pe, out_dve if s % 2 else out_act, 2 * q + s // 2)
                m_hi, m_lo = mix_hi[:, par, s, :], mix_lo[:, par, s, :]
                v_hi, v_lo = y_hi[:, par, :, s, :], y_lo[:, par, :, s, :]
                o = mix_ps[s % 2][:, :].rearrange("p (h j) -> p h j", h=QP)
                mm(o, m_hi, v_hi, start=True, stop=False)
                mm(o, m_lo, v_hi, start=False, stop=False)
                mm(o, m_hi, v_lo, start=False, stop=True).then_inc(mix_done, 1)

            pe.wait_ge(net_in, 16 * len(net_loads))
            pe.wait_ge(ones_set, 1)
            for n in range(NL):
                last = mm(bank[4][:, B * n:B * n + B], w0[:, n, :], cond[:], start=True, stop=True)
            last.then_inc(hid1_ps, 1)
            mm(bank[5][:, 0:C], cond[:], cw[:], start=True, stop=False)
            mm(bank[5][:, 0:C], ones[:], frow[:], start=False, stop=True).then_inc(c0_ps, 1)
            mm(bank[6][0:C, 0:B], cw[:], cond[:], start=True, stop=True).then_inc(c0_ps, 1)
            pe.wait_ge(toep_set, 1)
            conv(0, 0, 0, 0)
            pe.wait_ge(hid1_set, NL)
            for n in range(NL):
                last = mm(bank[7][:, B * n:B * n + B], w1[:, n, :], hid1[:, n, :], start=True, stop=True)
            last.then_inc(hid2_ps, 1)
            conv(0, 0, 0, 1)
            pe.wait_ge(hid2_set, NL)
            for n in range(NL):
                o = bank[4][:, K * n:K * n + K]
                mm(o, hid2[:, n, :], w2[:, n, :], start=True, stop=False)
                last = mm(o, ones[:], b2[:, K * n:K * n + K], start=False, stop=True)
            last.then_inc(logit_ps, 1)
            conv(0, 0, 0, 2)

            def bias_products(n):
                pe.wait_ge(c0_set if n == 0 else vcol_set, 2 if n == 0 else n)
                if n == 0:
                    pe.wait_ge(tab_in, 16 * len(tab_loads))
                mm(bank[5][:, :], vcol[:], mixrow[:, n, :], start=True, stop=False)
                mm(bank[5][:, :], ones[:], biask[:, n, :], start=False, stop=True).then_inc(prod_ps, 1)

            def bias_turn(n):
                pe.wait_ge(vrow_set, n + 1)
                nc.tensor.transpose(bank[5][0:C, 0:B], vrow[:], ident[:]).then_inc(vcol_ps, 1)

            bias_products(0)
            pe.wait_ge(att_set, 1)
            for n in range(NL):
                last = nc.tensor.transpose(bank[7][0:K, B * n:B * n + B], att[:, n, :], ident[:])
            last.then_inc(att_t_ps, 1)
            conv(0, 0, 0, 3)
            pe.wait_ge(att_t_set, 1)
            t_bank = [bank[4], bank[6], bank[7]]
            for t in range(NL * TG):
                n, c = divmod(t, TG)
                if t >= len(t_bank):
                    pe.wait_ge(tab_act, 2 * (t - len(t_bank) + 1))
                    pe.wait_ge(tab_dve, 2 * (t - len(t_bank) + 1))
                for i in range(NG):
                    last = mm(t_bank[t % 3][:, B * i:B * i + B], mixtab[:, n, NG * c + i, :], att_t[:, n, :],
                              start=True, stop=True)
                last.then_inc(tab_ps, 1)
                if t == 7:
                    bias_turn(0)
                if t == 10:
                    bias_products(1)
                if t == 15:
                    bias_turn(1)
                if t == 18:
                    bias_products(2)
            pe.wait_ge(vrow_set, NL)
            nc.tensor.transpose(bank[5][:, 0:B], vdup[:].rearrange("b g r o -> b (g r o)"),
                                ident[:]).then_inc(vcol_ps, 1)

            compose_lower(0, 0)
            compose_upper(0, 0)

            def step(q, it, par):
                if isinstance(q, int) and q == 1:
                    pe.wait_ge(vcol_set, NL)
                for qp in range(QP):
                    conv(q, it, par, qp)
                    if qp == 0:
                        compose_lower(q, par)
                    if qp == 2:
                        compose_upper(q, par)
                    mix(q - 1, 1 - par, qp)

            for q in range(1, PEEL):
                step(q, q // 2, q % 2)
            with pe.Fori(PEEL // 2, NQ // 2) as it:
                for par in range(2):
                    step(2 * it + par, it, par)
            for s in range(S):
                mix(NQ - 1, 1, s)

        @block.scalar
        def _(act):
            def y_high(q, par, qp):
                act.wait_ge(conv_done, 4 * q + qp + 1)
                if qp == 0:
                    wait(act, mix_done, 4 * q - 4)
                nc.scalar.activation(y_hi[:, par, qp], conv_ps[qp][:, :].rearrange("p (s j) -> p s j", s=S),
                                     ACT.Copy).then_inc(hi_done, 1)

            def a21_copy(q, par):
                act.wait_ge(a21_ps, q + 1)
                wait(act, comp_done, q - 1)
                for pr in range(PR):
                    src = pair_ps[:, C * pr:C * pr + C].rearrange("p (g o i) -> p g o i", g=G, o=1)
                    nc.scalar.activation(a21_dup[:, par, pr], src.to_broadcast([128, G, 2, CG]),
                                         ACT.Copy).then_inc(a21_set, 1)

            def mix_high(q, par):
                act.wait_ge(mixf_set, 2 * q + 2)
                nc.scalar.activation(mix_hi[:, par].rearrange("p s n -> p (s n)"),
                                     mix_f[:].rearrange("p a r o -> p (a r o)"), ACT.Copy).then_inc(mixhi_set, 1)

            def finish(q, it, par, s):
                act.wait_ge(mix_done, 4 * q + s + 1)
                if s == 0:
                    wait(act, stored[par], 16 * it)
                nc.scalar.activation(out_sb[:, par, s, :], mix_ps[s % 2][:, :], ACT.Identity,
                                     bias=beta[:, bass.ds(S * q + s, 1)]).then_inc(out_act, 1)

            act.wait_ge(hid1_ps, 1)
            for n in range(NL):
                nc.scalar.activation(hid1[:, n, :], bank[4][:, B * n:B * n + B], ACT.Gelu,
                                     bias=b01[:, 0, n:n + 1]).then_inc(hid1_set, 1)
            act.wait_ge(hid2_ps, 1)
            for n in range(NL):
                nc.scalar.activation(hid2[:, n, :], bank[7][:, B * n:B * n + B], ACT.Gelu,
                                     bias=b01[:, 1, n:n + 1]).then_inc(hid2_set, 1)
            y_high(0, 0, 0)
            act.wait_ge(centred, 1)
            nc.scalar.activation(expo[:], expo[:], ACT.Exp).then_inc(exp_set, 1)
            y_high(0, 0, 1)
            y_high(0, 0, 2)
            act.wait_ge(att_ones, 1)
            act.wait_ge(att_t_ps, 1)
            nc.scalar.activation(att_t[0:K, :, :], bank[7][0:K, 0:NL * B].rearrange("k (n b) -> k n b", n=NL),
                                 ACT.Copy).then_inc(att_t_set, 1)
            y_high(0, 0, 3)

            t_bank = [bank[4], bank[6], bank[7]]
            for t in range(NL * TG):
                n, c = divmod(t, TG)
                act.wait_ge(tab_ps, t + 1)
                src = t_bank[t % 3][0:C, :].rearrange("m (i p h) -> m p i h", i=NG, h=2)
                for h in range(2):
                    nc.scalar.activation(table[n][C * h:C * h + C, :, NG * c:NG * c + NG], src[:, :, :, h],
                                         ACT.Copy).then_inc(tab_act, 1)
                if t in (9, 17):
                    act.wait_ge(vcol_ps, 1 if t == 9 else 2)
                    nc.scalar.activation(vcol[:], bank[5][0:C, 0:B], ACT.Copy).then_inc(vcol_set, 1)
            act.wait_ge(vcol_ps, NL)
            nc.scalar.activation(beta[:], bank[5][:, 0:B], ACT.Copy).then_inc(vcol_set, 1)
            act.wait_ge(vcol_set, NL)
            a21_copy(0, 0)
            mix_high(0, 0)

            def step(q, it, par, itm):
                y_high(q, par, 0)
                a21_copy(q, par)
                finish(q - 1, itm, 1 - par, 0)
                y_high(q, par, 1)
                y_high(q, par, 2)
                mix_high(q, par)
                finish(q - 1, itm, 1 - par, 2)
                y_high(q, par, 3)

            for q in range(1, PEEL):
                step(q, q // 2, q % 2, (q - 1) // 2)
            with act.Fori(PEEL // 2, NQ // 2) as it:
                step(2 * it, it, 0, it - 1)
                step(2 * it + 1, it, 1, it)
            finish(NQ - 1, NQ // 2 - 1, 1, 0)
            finish(NQ - 1, NQ // 2 - 1, 1, 2)

        @block.vector
        def _(dve):
            def y_low(q, par, qp):
                dve.wait_ge(hi_done, 4 * q + qp + 1)
                if qp == 0:
                    wait(dve, mix_done, 4 * q - 4)
                nc.vector.tensor_tensor(y_lo[:, par, qp].rearrange("p s j -> p (s j)"), conv_ps[qp][:, :],
                                        y_hi[:, par, qp].rearrange("p s j -> p (s j)").bitcast(F32),
                                        ALU.subtract).then_inc(lo_done, 1)

            def mix_full(q):
                dve.wait_ge(comp_done, q + 1)
                src = comp_ps[:, 0:S * C].rearrange("p (a o) -> p a o", o=CG)
                for r in range(2):
                    nc.vector.tensor_scalar(mix_f[:, :, r, :], src, parity[:, r:r + 1], None,
                                            ALU.mult).then_inc(mixf_set, 1)

            def mix_low(q, par):
                dve.wait_ge(mixhi_set, q + 1)
                nc.vector.tensor_tensor(mix_lo[:, par].rearrange("p s n -> p (s n)"),
                                        mix_f[:].rearrange("p a r o -> p (a r o)"),
                                        mix_hi[:, par].rearrange("p s n -> p (s n)").bitcast(F32),
                                        ALU.subtract).then_inc(mixlo_set, 1)

            def finish(q, it, par, s):
                dve.wait_ge(mix_done, 4 * q + s + 1)
                if s == 1:
                    wait(dve, stored[par], 16 * it)
                nc.vector.tensor_scalar(out_sb[:, par, s, :], mix_ps[s % 2][:, :],
                                        beta[:, bass.ds(S * q + s, 1)], None, ALU.add).then_inc(out_dve, 1)

            dve.wait_ge(toep_in, 16 * len(toep_loads))
            own = toep[:, 0].rearrange("p g h m -> p g (h m)")
            nc.vector.tensor_tensor(own, own, eye_tap[:].unsqueeze(1).to_broadcast([128, G, QP * 32]),
                                    ALU.add).then_inc(toep_set, 1)
            dve.wait_ge(c0_ps, 2)
            nc.vector.tensor_copy(vrow[:], bank[5][:, 0:C]).then_inc(c0_set, 1)
            nc.vector.tensor_scalar(vcol[:], bank[6][0:C, 0:B], fcol[:], None, ALU.add).then_inc(c0_set, 1)
            y_low(0, 0, 0)
            logits = bank[4][:, 0:NL * K].rearrange("b (n k) -> b n k", n=NL)
            dve.wait_ge(logit_ps, 1)
            nc.vector.tensor_reduce(top[:], logits, AX_X, ALU.max).then_inc(softmax_chain, 1)
            dve.wait_ge(softmax_chain, 1)
            nc.vector.tensor_tensor(expo[:], logits, top[:].unsqueeze(2).to_broadcast([B, NL, K]),
                                    ALU.subtract).then_inc(centred, 1)
            dve.wait_ge(exp_set, 1)
            nc.vector.tensor_reduce(total[:], expo[:], AX_X, ALU.add).then_inc(softmax_chain, 1)
            dve.wait_ge(softmax_chain, 2)
            nc.vector.reciprocal(recip[:], total[:]).then_inc(softmax_chain, 1)
            dve.wait_ge(softmax_chain, 3)
            nc.vector.tensor_tensor(att[:], expo[:], recip[:].unsqueeze(2).to_broadcast([B, NL, K]),
                                    ALU.mult).then_inc(att_set, 1)
            y_low(0, 0, 1)
            y_low(0, 0, 2)
            y_low(0, 0, 3)

            def bias_sum(n):
                dve.wait_ge(prod_ps, n + 1)
                if n == 0:
                    dve.wait_ge(att_set, 1)
                for k in range(K):
                    if n + k:
                        dve.wait_ge(bias_chain, n * K + k)
                    ins = nc.vector.scalar_tensor_tensor(
                        out=vrow[:], in0=bank[5][:, C * k:C * k + C], scalar=att[:, n, k:k + 1], in1=vrow[:],
                        op0=ALU.mult, op1=ALU.add).then_inc(bias_chain, 1)
                dve.wait_ge(bias_chain, n * K + K)
                if n < NL - 1:
                    nc.vector.tensor_copy(top[:, 0:1], vrow[:, 0:1]).then_inc(vrow_set, 1)
                else:
                    src = vrow[:].rearrange("b (g o i) -> b g o i", g=G, o=1)
                    nc.vector.tensor_copy(vdup[:], src.to_broadcast([B, G, 2, CG])).then_inc(vrow_set, 1)

            bias_sum(0)
            t_bank = [bank[4], bank[6], bank[7]]
            for t in range(NL * TG):
                n, c = divmod(t, TG)
                dve.wait_ge(tab_ps, t + 1)
                src = t_bank[t % 3][C:2 * C, :].rearrange("m (i p h) -> m p i h", i=NG, h=2)
                for h in range(2):
                    nc.vector.tensor_copy(table[n][C * h:C * h + C, :, NH + NG * c:NH + NG * c + NG],
                                          src[:, :, :, h]).then_inc(tab_dve, 1)
                if t == 12:
                    bias_sum(1)
                if t == 20:
                    bias_sum(2)
            mix_full(0)
            mix_low(0, 0)
            dve.wait_ge(vcol_set, NL)

            def step(q, it, par, itm):
                y_low(q, par, 0)
                y_low(q, par, 1)
                finish(q - 1, itm, 1 - par, 1)
                mix_full(q)
                y_low(q, par, 2)
                mix_low(q, par)
                y_low(q, par, 3)
                finish(q - 1, itm, 1 - par, 3)

            for q in range(1, PEEL):
                step(q, q // 2, q % 2, (q - 1) // 2)
            with dve.Fori(PEEL // 2, NQ // 2) as it:
                step(2 * it, it, 0, it - 1)
                step(2 * it + 1, it, 1, it)
            finish(NQ - 1, NQ // 2 - 1, 1, 1)
            finish(NQ - 1, NQ // 2 - 1, 1, 3)


def toeplitz(weight):
    w = weight.reshape(G, CG, CG, TAPS)
    out = np.zeros((CG, PH, 2, G, QP, 2, CG), weight.dtype)
    for p in range(PH):
        for n in range(PH):
            for side in range(2):
                shift = 0 if side == 0 else (-PH if n < PH // 2 else PH)
                tap = p + shift - n + PAD
                if 0 <= tap < TAPS:
                    out[:, p, side, :, n // 2, n % 2, :] = w[:, :, :, tap].transpose(2, 0, 1)
    return out.reshape(128, 2, G, QP, 2 * CG)


def kernel(**inputs):
    import concourse.bacc as bacc
    from concourse.bass_utils import run_bass_kernel_spmd

    a = {k: np.asarray(v) for k, v in inputs.items()}
    f = np.float32
    mixes = [f"L{n}_cond_" for n in (1, 2, 3)]

    x = a["x"].reshape(NQ, S, G, CG, J, PH).transpose(0, 3, 5, 2, 1, 4).reshape(NQ * 128, G * N)
    eye_tap = np.zeros((CG, PH, QP, 2, CG), f)
    for c in range(CG):
        for p in range(PH):
            eye_tap[c, p, p // 2, p % 2, c] = 1
    parity = np.zeros((G, 2, CG, 2), f)
    parity[:, 0, :, 0] = 1
    parity[:, 1, :, 1] = 1
    eye = np.eye(C, dtype=f)

    def table_rows(w, m_is_out):
        w = np.concatenate([w, eye[None], np.zeros((KP - K - 1, C, C), f)])
        w = w if m_is_out else w.transpose(0, 2, 1)
        return w.reshape(KP, C, 2, NH).transpose(0, 3, 2, 1).reshape(KP, NH, 2 * C)

    ws = [a[p + "weight"].reshape(K, C, C) for p in mixes]
    arrays = {
        "x": x,
        "toep": toeplitz(a["L0_cond_weight"]),
        "eye_tap": eye_tap.reshape(128, QP * 32),
        "cond_t": a["cond_128"].T,
        "w0": np.stack([a[p + "W0"] for p in mixes], 1),
        "w1": np.stack([a[p + "W1"] for p in mixes], 1),
        "w2": np.stack([a[p + "W2"] for p in mixes], 1),
        "b01": np.stack([np.stack([a[p + b] for p in mixes], 1) for b in ("b0", "b1")], 1),
        "b2": np.concatenate([a[p + "b2"] for p in mixes])[None],
        "cw": a["L0_cond_c_weight"].T,
        "fs_col": a["fside_S_0"][:, None],
        "fs_row": a["fside_S_0"][None],
        "mixrow": np.stack([w.transpose(2, 0, 1).reshape(C, K * C) for w in ws], 1),
        "biask": np.stack([a[p + "bias_k"].reshape(K * C) for p in mixes])[None],
        "mixtab": np.stack([table_rows(w, n == 0) for n, w in enumerate(ws)], 1),
        "ident": np.eye(128, dtype=f),
        "parity": parity.reshape(128, 2),
    }
    nc = bacc.Bacc("TRN2", target_bir_lowering=False, num_devices=1)
    sent, args = {}, []
    for name, v in arrays.items():
        v = np.ascontiguousarray(v)
        sent[f"in_{name}"] = v
        args.append(nc.dram_tensor(f"in_{name}", v.shape, mybir.dt.from_np(v.dtype), kind="ExternalInput").ap())
    args.append(nc.dram_tensor("out", (NQ * 128, S * QP * J), F32, kind="ExternalOutput").ap())
    cond_resid_kernel(nc, *args)
    got = run_bass_kernel_spmd(nc, [sent], core_ids=[0]).results[0]["out"]
    return got.reshape(NQ, G, 2, CG, S, QP, J).transpose(0, 4, 1, 3, 6, 5, 2).reshape(B, C, L)
```

```python
from contextlib import ExitStack

import numpy as np

import concourse.bass as bass
from concourse import mybir

F32 = mybir.dt.float32
F32R = mybir.dt.float32r
ALU = mybir.AluOpType
ACT = mybir.ActivationFunctionType
AX_X = mybir.AxisListType.X

B, C, L = 128, 64, 1024
G, CG = 4, 16
TAPS, PAD = 9, 4
PH = 8
J = L // PH
QP = PH // 2
JX = J + 1
S = 4
NQ = B // S
PR = S // 2
D = 128
K = 8
KR = K + 1
PARTS = 4
NL = 3
N = S * J
NH = C // 2
NG = 4
TG = NH // NG
NTAB = NL * TG
BIAS_TURNS = (5, 13)
BIAS_PRODUCTS = (7, 15)
CONV_AFTER = {3: (1, 0), 6: (1, 1), 9: (1, 2), 12: (1, 3), 16: (2, 0), 20: (2, 1)}
CH = 12
CW = NL * NH * 2 * C // CH
NET = dict(cond=B, w0=NL * D, b01=2 * NL, cw=C, fcol=1, w1=NL * D, w2=NL * K)
KEPT = dict(ident=128, parity=2)
ROW = dict(frow=C, b2=NL * K)
TOEP = dict(toep=2 * G * 128, eye_tap=2 * 128)


def columns(tile, widths):
    out, at = {}, 0
    for name, n in widths.items():
        out[name] = tile[:, at:at + n]
        at += n
    return out


def cond_resid_kernel(nc, x_h, net_h, kept_h, row_h, toep_h, mixrow_h, mats_h, out_h):
    with ExitStack() as ctx:
        def sb(name, shape, dt=F32):
            return ctx.enter_context(nc.sbuf_tensor(name, shape, dt))

        def sem(name):
            return ctx.enter_context(nc.semaphore(name))

        bank = [ctx.enter_context(nc.psum_tensor(f"bank{i}", [128, 512], F32)) for i in range(8)]
        conv_ps, mix_ps = bank[0:4], bank[4:6]
        pair_ps, comp_ps = bank[6], bank[7]

        table = [sb(f"table{n}", [128, B // 2, C]) for n in range(NL)]
        early = columns(table[2][:].rearrange("p b c -> p (b c)"), dict(net=sum(NET.values()), mixrow=NL * K * C))
        net = early["net"]
        mixrow = early["mixrow"][0:C + 1].rearrange("p (n m) -> p n m", n=NL)
        kept = sb("kept", [128, sum(KEPT.values())])
        row = sb("row", [1, sum(ROW.values())])
        part = columns(net, NET)
        cond, cw = part["cond"], part["cw"]
        ident, parity = columns(kept, KEPT).values()
        w0, w1, w2 = (part[n].rearrange("p (n m) -> p n m", n=NL) for n in ("w0", "w1", "w2"))
        b01 = part["b01"].rearrange("p (t n) -> p t n", t=2)
        fcol = part["fcol"][0:C, :]
        frow, b2 = columns(row, ROW).values()
        toep_hi = sb("toep_hi", [128, 2, G, 128], F32R)
        toep_lo = sb("toep_lo", [128, 2, G, 128], F32R)
        mixtab = sb("mixtab", [128, NL, NH, 2 * C], F32R)
        ones = sb("ones", [1, B])
        top = sb("top", [B, NL])
        expo = sb("expo", [B, NL, K])
        total = sb("total", [B, NL])
        recip = sb("recip", [B, NL])
        att = sb("att", [B, NL, K])
        att_pad = sb("att_pad", [B, NL, 128], F32R)
        att_parts = att_pad[:, :, 0:PARTS * KR].rearrange("b n (t k) -> b n t k", t=PARTS)
        att_t = sb("att_t", [128, NL, B], F32R)
        vrow = sb("vrow", [B, C])
        vcol = sb("vcol", [C + 1, B])
        vdup = sb("vdup", [B, G, 2, CG])
        beta = sb("beta", [128, B])

        x_sb = sb("x_sb", [128, 2, G, S, JX])
        x_hi = sb("x_hi", [128, 2, G, S, JX], F32R)
        x_lo = sb("x_lo", [128, 2, G, S, JX], F32R)
        conv_sb = sb("conv_sb", [128, 2, G, N])
        out_sb = sb("out_sb", [128, 2, S, QP * J])
        y_sb, y_hi, y_lo = (mixtab[:, n].rearrange("p (r h s) j -> p r h s j", r=2, h=QP) for n in range(NL))
        y_sb = y_sb.bitcast(F32)
        mats = x_sb[:, 1].rearrange("p g s j -> p (g s j)")[0:KR * CH, 0:CW]
        mats_hi = conv_sb[:, 1].rearrange("p g n -> p (g n)")[0:KR * CH, 0:CW].bitcast(F32R)
        mats_lo = out_sb[:, 0].rearrange("p s n -> p (s n)")[0:KR * CH, 0:CW].bitcast(F32R)
        second = columns(out_sb[:, 1].rearrange("p s n -> p (s n)"), dict(TOEP, hid1=NL * B, hid2=NL * B))
        toep, eye_tap = second["toep"], second["eye_tap"]
        toep_all = out_sb[:, 1].rearrange("p s n -> p (s n)")[:, 0:sum(TOEP.values())]
        hid1, hid2 = (second[n].rearrange("p (n b) -> p n b", n=NL) for n in ("hid1", "hid2"))
        a1_pair = sb("a1_pair", [128, 2, PR, C])
        a2_diag = sb("a2_diag", [128, 2, PR, 2 * C])
        a3_diag = sb("a3_diag", [128, 2, PR, 2 * C])
        a21_dup = sb("a21_dup", [128, 2, PR, G, 2, CG])
        mix_f = sb("mix_f", [128, S * G, 2, CG])
        mix_hi = sb("mix_hi", [128, 2, S, 128], F32R)
        mix_lo = sb("mix_lo", [128, 2, S, 128], F32R)

        net_in, kept_in, toep_in, mats_in, mixrow_in, tab_in = (
            sem(n) for n in ("net_in", "kept_in", "toep_in", "mats_in", "mixrow_in", "tab_in"))
        mats_hi_set, mats_lo_set, parts_zero, parts_set = (
            sem(n) for n in ("mats_hi_set", "mats_lo_set", "parts_zero", "parts_set"))
        mixtab_zero = sem("mixtab_zero")
        x_in = [sem("x_in0"), sem("x_in1")]
        stored = [sem("stored0"), sem("stored1")]
        ones_set, toep_set, zeros_set = sem("ones_set"), sem("toep_set"), sem("zeros_set")
        hid1_ps, hid1_set, hid2_ps, hid2_set = sem("hid1_ps"), sem("hid1_set"), sem("hid2_ps"), sem("hid2_set")
        c0_ps, c0_set = sem("c0_ps"), sem("c0_set")
        logit_ps, centred, exp_set, att_set = sem("logit_ps"), sem("centred"), sem("exp_set"), sem("att_set")
        softmax_chain, bias_chain = sem("softmax_chain"), sem("bias_chain")
        att_t_ps, att_t_set = sem("att_t_ps"), sem("att_t_set")
        prod_ps, vrow_set, vcol_ps, vcol_set = sem("prod_ps"), sem("vrow_set"), sem("vcol_ps"), sem("vcol_set")
        tab_ps, tab_act, tab_dve = sem("tab_ps"), sem("tab_act"), sem("tab_dve")
        toep_hi_set, toep_lo_set = sem("toep_hi_set"), sem("toep_lo_set")
        xhi_set, xlo_set, conv_done, conv_out = (sem(n) for n in ("xhi_set", "xlo_set", "conv_done", "conv_out"))
        moved = [sem("moved0"), sem("moved1")]
        yhi_set, ylo_set, a3_in = sem("yhi_set"), sem("ylo_set"), sem("a3_in")
        pair_in, a21_ps, a21_set, comp_done = sem("pair_in"), sem("a21_ps"), sem("a21_set"), sem("comp_done")
        mixf_set, mixhi_set, mixlo_set = sem("mixf_set"), sem("mixhi_set"), sem("mixlo_set")
        mix_done, out_act, out_dve = sem("mix_done"), sem("out_act"), sem("out_dve")

        def shared(t):
            return t % 4 != 3

        def dve_banks(t):
            return sum(shared(u) for u in range(t))

        PEEL = 4

        def wait(eng, s, value):
            if not isinstance(value, int) or value > 0:
                eng.wait_ge(s, value)

        block = ctx.enter_context(nc.Block())

        @block.sync
        def _(sp):
            def load(q, par):
                sp.dma_start(x_sb[:, par].rearrange("p g s j -> p (g s j)"),
                             x_h[bass.ds(q * 128, 128), :]).then_inc(x_in[par], 16)

            def store(q, par):
                sp.wait_ge(out_act, 2 * q + 2)
                sp.wait_ge(out_dve, 2 * q + 2)
                sp.dma_start(out_h[bass.ds(q * 128, 128), :],
                             out_sb[:, par].rearrange("p s n -> p (s n)")).then_inc(stored[par], 16)

            def move(q, par, g):
                if g == 0:
                    wait(sp, ylo_set, q - 1)
                sp.wait_ge(conv_out, 4 * q + g + 1)
                sp.dma_start(y_sb[32 * g:32 * g + 32, par].rearrange("p h s j -> p h (s j)"),
                             conv_sb[:, par, g, :]).then_inc(moved[par], 16)

            sp.dma_start(net, net_h).then_inc(net_in, 16)
            sp.dma_start(kept[:], kept_h).then_inc(kept_in, 16)
            sp.dma_start(row[:], row_h).then_inc(net_in, 16)
            sp.dma_start(toep_all, toep_h).then_inc(toep_in, 16)
            sp.dma_start(mats, mats_h).then_inc(mats_in, 16)
            load(0, 0)
            sp.dma_start(mixrow, mixrow_h).then_inc(mixrow_in, 16)
            sp.wait_ge(mixtab_zero, 2)
            for i, (src, ready) in enumerate(((mats_hi, mats_hi_set), (mats_lo, mats_lo_set))):
                sp.wait_ge(ready, 1)
                for j in range(2):
                    rows = slice(KR * (2 * i + j), KR * (2 * i + j + 1))
                    dst = mixtab[rows].rearrange("k n c m -> k (n c m)").rearrange("k (c n) -> k c n", c=CH)
                    sp.dma_start(dst.bitcast(F32), src.bitcast(F32)).then_inc(tab_in, 16)
            load(1, 1)
            sp.wait_ge(xhi_set, 1)
            sp.wait_ge(xlo_set, 1)
            load(2, 0)
            sp.wait_ge(tab_ps, TG)
            for g in range(G):
                move(0, 0, g)

            def step(q, par):
                if not isinstance(q, int) or q + 2 < NQ:
                    sp.wait_ge(xhi_set, q + 1)
                    sp.wait_ge(xlo_set, q + 1)
                    load(q + 2, par)
                move(q, par, 0)
                if not isinstance(q, int) or q >= 3:
                    store(q - 3, 1 - par)
                for g in range(1, G):
                    move(q, par, g)

            for q in range(1, PEEL):
                step(q, q % 2)
            with sp.Fori(PEEL // 2, NQ // 2 - 1) as it:
                step(2 * it, 0)
                step(2 * it + 1, 1)
            step(NQ - 2, 0)
            step(NQ - 1, 1)
            for q in range(NQ - 3, NQ):
                store(q, q % 2)
            for par in range(2):
                sp.wait_ge(stored[par], 16 * (NQ // 2))

        @block.gpsimd
        def _(pool):
            nc.gpsimd.memset(mixtab[:, 1:].bitcast(F32), 0.0).then_inc(mixtab_zero, 1)
            nc.gpsimd.memset(ones[:], 1.0).then_inc(ones_set, 1)
            nc.gpsimd.memset(vcol[:], 1.0).then_inc(ones_set, 1)
            nc.gpsimd.memset(att_pad[:].bitcast(F32), 0.0).then_inc(parts_zero, 1)
            pool.wait_ge(parts_zero, 1)
            nc.gpsimd.memset(att_parts[:, :, 0::2, K:KR].bitcast(F32), 1.0).then_inc(parts_zero, 1)
            nc.gpsimd.memset(a2_diag[:], 0.0).then_inc(zeros_set, 1)
            nc.gpsimd.memset(a3_diag[:], 0.0).then_inc(zeros_set, 1)
            pool.wait_ge(zeros_set, 2)

            def lower_mats(q, par):
                wait(pool, a21_ps, q - 1)
                wait(pool, a3_in, 2 * q if not isinstance(q, int) or q > 1 else 0)
                here = bass.ds(PR * q, PR)
                wait(pool, pair_in, 3 * q)
                nc.gpsimd.tensor_copy(a1_pair[:, par], table[0][:, here, :]).then_inc(pair_in, 1)
                for h in range(2):
                    rows = slice(C * h, C * h + C)
                    pool.wait_ge(pair_in, 3 * q + h + 1)
                    nc.gpsimd.tensor_copy(a2_diag[rows, par, :, C * h:C * h + C],
                                          table[1][rows, here, :]).then_inc(pair_in, 1)

            def upper_mats(q, par):
                wait(pool, comp_done, q - 1)
                pool.wait_ge(pair_in, 3 * q + 3)
                here = bass.ds(PR * q, PR)
                for h in range(2):
                    rows = slice(C * h, C * h + C)
                    wait(pool, a3_in, 2 * q + h)
                    nc.gpsimd.tensor_copy(a3_diag[rows, par, :, C * h:C * h + C],
                                          table[2][rows, here, :]).then_inc(a3_in, 1)

            def tables_full(t):
                pool.wait_ge(tab_act, t)
                pool.wait_ge(tab_dve, dve_banks(t))

            tables_full(2 * TG)
            lower_mats(0, 0)
            lower_mats(1, 1)
            pool.wait_ge(pair_in, 6)
            tables_full(NTAB)
            upper_mats(0, 0)
            upper_mats(1, 1)

            def step(q, par):
                lower_mats(q, par)
                upper_mats(q, par)

            for q in range(2, PEEL):
                step(q, q % 2)
            with pool.Fori(PEEL // 2, NQ // 2) as it:
                step(2 * it, 0)
                step(2 * it + 1, 1)

        @block.tensor
        def _(pe):
            mm = nc.tensor.matmul

            def conv(q, par, g):
                if g == 0:
                    pe.wait_ge(xhi_set, q + 1)
                    pe.wait_ge(xlo_set, q + 1)
                wait(pe, conv_out, 4 * q + g - 3)
                o = conv_ps[g][:, :].rearrange("p (s j) -> p s j", s=S)
                for i, (w, v) in enumerate(((toep_hi, x_hi), (toep_lo, x_hi), (toep_hi, x_lo))):
                    for d in range(2):
                        last = mm(o, w[:, d, g, :], v[:, par, g, :, d:d + J], start=i + d == 0, stop=i + d == 3)
                last.then_inc(conv_done, 1)

            def compose_lower(q, par):
                pe.wait_ge(pair_in, 3 * q + 3)
                wait(pe, a21_set, 2 * q)
                for pr in range(PR):
                    last = mm(pair_ps[:, C * pr:C * pr + C], a2_diag[:, par, pr, :], a1_pair[:, par, pr, :],
                              start=True, stop=True)
                last.then_inc(a21_ps, 1)

            def compose_upper(q, par):
                pe.wait_ge(a21_set, 2 * q + 2)
                pe.wait_ge(a3_in, 2 * q + 2)
                wait(pe, mixf_set, 2 * q)
                for pr in range(PR):
                    last = mm(comp_ps[:, 128 * pr:128 * pr + 128],
                              a21_dup[:, par, pr].rearrange("p g r i -> p (g r i)"), a3_diag[:, par, pr, :],
                              start=True, stop=True)
                last.then_inc(comp_done, 1)

            def mix(q, par, s):
                if s == 0:
                    pe.wait_ge(yhi_set, q + 1)
                    pe.wait_ge(ylo_set, q + 1)
                    pe.wait_ge(mixlo_set, q + 1)
                wait(pe, out_dve if s % 2 else out_act, 2 * q + s // 2)
                m_hi, m_lo = mix_hi[:, par, s, :], mix_lo[:, par, s, :]
                v_hi, v_lo = y_hi[:, par, :, s, :], y_lo[:, par, :, s, :]
                o = mix_ps[s % 2][:, :].rearrange("p (h j) -> p h j", h=QP)
                mm(o, m_hi, v_hi, start=True, stop=False)
                mm(o, m_lo, v_hi, start=False, stop=False)
                mm(o, m_hi, v_lo, start=False, stop=True).then_inc(mix_done, 1)

            pe.wait_ge(net_in, 32)
            pe.wait_ge(ones_set, 2)
            for n in range(NL):
                last = mm(bank[4][:, B * n:B * n + B], w0[:, n, :], cond, start=True, stop=True)
            last.then_inc(hid1_ps, 1)
            mm(bank[5][:, 0:C], cond, cw, start=True, stop=False)
            mm(bank[5][:, 0:C], ones[:], frow, start=False, stop=True).then_inc(c0_ps, 1)
            mm(bank[6][0:C, 0:B], cw, cond, start=True, stop=True).then_inc(c0_ps, 1)
            pe.wait_ge(hid1_set, NL)
            for n in range(NL):
                last = mm(bank[7][:, B * n:B * n + B], w1[:, n, :], hid1[:, n, :], start=True, stop=True)
            last.then_inc(hid2_ps, 1)
            pe.wait_ge(hid2_set, NL)
            for n in range(NL):
                o = bank[4][:, K * n:K * n + K]
                mm(o, hid2[:, n, :], w2[:, n, :], start=True, stop=False)
                last = mm(o, ones[:], b2[:, K * n:K * n + K], start=False, stop=True)
            last.then_inc(logit_ps, 1)
            pe.wait_ge(toep_hi_set, 1)
            pe.wait_ge(toep_lo_set, 1)
            conv(0, 0, 0)
            conv(0, 0, 1)

            def bias_products(n):
                if n == 0:
                    pe.wait_ge(mixrow_in, 16)
                    pe.wait_ge(c0_set, 2)
                else:
                    pe.wait_ge(vcol_set, n)
                mm(bank[5][:, :], vcol[:], mixrow[:, n, :], start=True, stop=True).then_inc(prod_ps, 1)

            def bias_turn(n):
                pe.wait_ge(vrow_set, n + 1)
                nc.tensor.transpose(bank[5][0:C, 0:B], vrow[:], ident).then_inc(vcol_ps, 1)

            bias_products(0)
            pe.wait_ge(parts_set, 2)
            pe.wait_ge(kept_in, 16)
            for n in range(NL):
                last = nc.tensor.transpose(bank[7][:, B * n:B * n + B], att_pad[:, n, :].bitcast(F32), ident)
            last.then_inc(att_t_ps, 1)
            conv(0, 0, 2)
            conv(0, 0, 3)
            pe.wait_ge(att_t_set, 1)
            pe.wait_ge(tab_in, 16 * PARTS)
            t_bank = [bank[4], bank[6], bank[7]]
            for t in range(NTAB):
                n, c = divmod(t, TG)
                if t >= len(t_bank):
                    pe.wait_ge(tab_act, t - len(t_bank) + 1)
                    pe.wait_ge(tab_dve, dve_banks(t - len(t_bank) + 1))
                for i in range(NG):
                    last = mm(t_bank[t % 3][:, B * i:B * i + B], mixtab[:, n, NG * c + i, :], att_t[:, n, :],
                              start=True, stop=True)
                last.then_inc(tab_ps, 1)
                if t in CONV_AFTER:
                    q, g = CONV_AFTER[t]
                    conv(q, q % 2, g)
                if t == BIAS_TURNS[0]:
                    bias_turn(0)
                if t == BIAS_PRODUCTS[0]:
                    bias_products(1)
                if t == BIAS_TURNS[1]:
                    bias_turn(1)
                if t == BIAS_PRODUCTS[1]:
                    bias_products(2)
            pe.wait_ge(vrow_set, NL)
            nc.tensor.transpose(bank[5][:, 0:B], vdup[:].rearrange("b g r o -> b (g r o)"),
                                ident).then_inc(vcol_ps, 1)
            conv(2, 0, 2)
            conv(2, 0, 3)

            pe.wait_ge(tab_act, NTAB)
            pe.wait_ge(tab_dve, dve_banks(NTAB))
            compose_lower(0, 0)
            compose_upper(0, 0)
            compose_lower(1, 1)
            mix(0, 0, 0)
            pe.wait_ge(vcol_set, NL)
            mix(0, 0, 1)
            compose_upper(1, 1)
            mix(0, 0, 2)
            mix(0, 0, 3)

            def step(q, par):
                for g in range(G):
                    conv(q, par, g)
                    if g == 0:
                        compose_lower(q - 1, 1 - par)
                    mix(q - 2, par, g)
                    if g == 1:
                        compose_upper(q - 1, 1 - par)

            step(3, 1)
            with pe.Fori(PEEL // 2, NQ // 2) as it:
                step(2 * it, 0)
                step(2 * it + 1, 1)
            compose_lower(NQ - 1, 1)
            for s in range(S // 2):
                mix(NQ - 2, 0, s)
            compose_upper(NQ - 1, 1)
            for s in range(S // 2, S):
                mix(NQ - 2, 0, s)
            for s in range(S):
                mix(NQ - 1, 1, s)

        @block.scalar
        def _(act):
            def x_high(q, it, par):
                act.wait_ge(x_in[par], 16 * it + 16)
                wait(act, conv_done, 4 * q - 4)
                nc.scalar.activation(x_hi[:, par].rearrange("p g s j -> p (g s j)"),
                                     x_sb[:, par].rearrange("p g s j -> p (g s j)"), ACT.Copy).then_inc(xhi_set, 1)

            def conv_copy(q, it, par, g):
                act.wait_ge(conv_done, 4 * q + g + 1)
                if g == 0:
                    wait(act, moved[par], 16 * G * it)
                nc.scalar.activation(conv_sb[:, par, g, :], conv_ps[g][:, :], ACT.Copy).then_inc(conv_out, 1)

            def a21_copy(q, par):
                act.wait_ge(a21_ps, q + 1)
                wait(act, comp_done, q - 1)
                for pr in range(PR):
                    src = pair_ps[:, C * pr:C * pr + C].rearrange("p (g o i) -> p g o i", g=G, o=1)
                    nc.scalar.activation(a21_dup[:, par, pr], src.to_broadcast([128, G, 2, CG]),
                                         ACT.Copy).then_inc(a21_set, 1)

            def mix_high(q, par):
                act.wait_ge(mixf_set, 2 * q + 2)
                nc.scalar.activation(mix_hi[:, par].rearrange("p s n -> p (s n)"),
                                     mix_f[:].rearrange("p a r o -> p (a r o)"), ACT.Copy).then_inc(mixhi_set, 1)

            def finish(q, it, par, s):
                act.wait_ge(mix_done, 4 * q + s + 1)
                if s == 0:
                    wait(act, stored[par], 16 * it)
                nc.scalar.activation(out_sb[:, par, s, :], mix_ps[s % 2][:, :], ACT.Identity,
                                     bias=beta[:, bass.ds(S * q + s, 1)]).then_inc(out_act, 1)

            act.wait_ge(hid1_ps, 1)
            for n in range(NL):
                nc.scalar.activation(hid1[:, n, :], bank[4][:, B * n:B * n + B], ACT.Gelu,
                                     bias=b01[:, 0, n:n + 1]).then_inc(hid1_set, 1)
            act.wait_ge(toep_set, 1)
            nc.scalar.activation(toep_hi[:].rearrange("p d g m -> p (d g m)"), toep,
                                 ACT.Copy).then_inc(toep_hi_set, 1)
            act.wait_ge(hid2_ps, 1)
            for n in range(NL):
                nc.scalar.activation(hid2[:, n, :], bank[7][:, B * n:B * n + B], ACT.Gelu,
                                     bias=b01[:, 1, n:n + 1]).then_inc(hid2_set, 1)
            act.wait_ge(mats_in, 16)
            nc.scalar.activation(mats_hi, mats, ACT.Copy).then_inc(mats_hi_set, 1)
            x_high(0, 0, 0)
            act.wait_ge(centred, 1)
            nc.scalar.activation(expo[:], expo[:], ACT.Exp).then_inc(exp_set, 1)
            conv_copy(0, 0, 0, 0)
            conv_copy(0, 0, 0, 1)
            act.wait_ge(att_t_ps, 1)
            nc.scalar.activation(att_t[:], bank[7][:, 0:NL * B].rearrange("k (n b) -> k n b", n=NL),
                                 ACT.Copy).then_inc(att_t_set, 1)
            conv_copy(0, 0, 0, 2)
            conv_copy(0, 0, 0, 3)
            x_high(1, 0, 1)

            def table_bank(t):
                n, c = divmod(t, TG)
                act.wait_ge(tab_ps, t + 1)
                for half in range(1 if shared(t) else 2):
                    src = t_bank[t % 3][C * half:C * half + C, :].rearrange("m (i p h) -> m p i h", i=NG, h=2)
                    at = NH * half + NG * c
                    for h in range(2):
                        last = nc.scalar.activation(table[n][C * h:C * h + C, :, at:at + NG],
                                                    src[:, :, :, h], ACT.Copy)
                last.then_inc(tab_act, 1)

            t_bank = [bank[4], bank[6], bank[7]]
            for t in range(NTAB):
                table_bank(t)
                if t - 1 in CONV_AFTER:
                    q, g = CONV_AFTER[t - 1]
                    conv_copy(q, q // 2, q % 2, g)
                if t == TG:
                    x_high(2, 1, 0)
                if t - 1 in BIAS_TURNS:
                    act.wait_ge(vcol_ps, BIAS_TURNS.index(t - 1) + 1)
                    nc.scalar.activation(vcol[0:C, :], bank[5][0:C, 0:B], ACT.Copy).then_inc(vcol_set, 1)
            a21_copy(0, 0)
            conv_copy(2, 1, 0, 2)
            conv_copy(2, 1, 0, 3)
            act.wait_ge(vcol_ps, NL)
            nc.scalar.activation(beta[:], bank[5][:, 0:B], ACT.Copy).then_inc(vcol_set, 1)
            x_high(3, 1, 1)
            mix_high(0, 0)
            a21_copy(1, 1)
            act.wait_ge(vcol_set, NL)
            finish(0, 0, 0, 0)
            mix_high(1, 1)
            finish(0, 0, 0, 2)

            def step(q, it, par, it_next):
                if not isinstance(q, int) or q + 1 < NQ:
                    x_high(q + 1, it_next, 1 - par)
                conv_copy(q, it, par, 0)
                a21_copy(q - 1, 1 - par)
                finish(q - 2, it - 1, par, 0)
                conv_copy(q, it, par, 1)
                conv_copy(q, it, par, 2)
                mix_high(q - 1, 1 - par)
                finish(q - 2, it - 1, par, 2)
                conv_copy(q, it, par, 3)

            step(3, 1, 1, 2)
            with act.Fori(PEEL // 2, NQ // 2 - 1) as it:
                step(2 * it, it, 0, it)
                step(2 * it + 1, it, 1, it + 1)
            step(NQ - 2, NQ // 2 - 1, 0, NQ // 2 - 1)
            step(NQ - 1, NQ // 2 - 1, 1, NQ // 2)
            a21_copy(NQ - 1, 1)
            finish(NQ - 2, NQ // 2 - 1, 0, 0)
            mix_high(NQ - 1, 1)
            finish(NQ - 2, NQ // 2 - 1, 0, 2)
            finish(NQ - 1, NQ // 2 - 1, 1, 0)
            finish(NQ - 1, NQ // 2 - 1, 1, 2)

        @block.vector
        def _(dve):
            def x_low(q, par):
                dve.wait_ge(xhi_set, q + 1)
                wait(dve, conv_done, 4 * q - 4)
                nc.vector.tensor_tensor(x_lo[:, par].rearrange("p g s j -> p (g s j)"),
                                        x_sb[:, par].rearrange("p g s j -> p (g s j)"),
                                        x_hi[:, par].rearrange("p g s j -> p (g s j)").bitcast(F32),
                                        ALU.subtract).then_inc(xlo_set, 1)

            def y_high(q, it, par):
                dve.wait_ge(moved[par], 16 * G * it + 16 * G)
                wait(dve, mix_done, 4 * q - 4)
                v, hi = (t[:, par].rearrange("p h s j -> p (h s j)") for t in (y_sb, y_hi))
                nc.vector.tensor_copy(hi, v).then_inc(yhi_set, 1)

            def y_low(q, par):
                dve.wait_ge(yhi_set, q + 1)
                v, hi, lo = (t[:, par].rearrange("p h s j -> p (h s j)") for t in (y_sb, y_hi, y_lo))
                nc.vector.tensor_tensor(lo, v, hi.bitcast(F32), ALU.subtract).then_inc(ylo_set, 1)

            def mix_full(q):
                dve.wait_ge(comp_done, q + 1)
                src = comp_ps[:, 0:S * C].rearrange("p (a o) -> p a o", o=CG)
                for r in range(2):
                    nc.vector.tensor_scalar(mix_f[:, :, r, :], src, parity[:, r:r + 1], None,
                                            ALU.mult).then_inc(mixf_set, 1)

            def mix_low(q, par):
                dve.wait_ge(mixhi_set, q + 1)
                nc.vector.tensor_tensor(mix_lo[:, par].rearrange("p s n -> p (s n)"),
                                        mix_f[:].rearrange("p a r o -> p (a r o)"),
                                        mix_hi[:, par].rearrange("p s n -> p (s n)").bitcast(F32),
                                        ALU.subtract).then_inc(mixlo_set, 1)

            def finish(q, it, par, s):
                dve.wait_ge(mix_done, 4 * q + s + 1)
                if s == 1:
                    wait(dve, stored[par], 16 * it)
                nc.vector.tensor_scalar(out_sb[:, par, s, :], mix_ps[s % 2][:, :],
                                        beta[:, bass.ds(S * q + s, 1)], None, ALU.add).then_inc(out_dve, 1)

            def bias_sum(n):
                dve.wait_ge(prod_ps, n + 1)
                if n == 0:
                    dve.wait_ge(att_set, 1)
                for k in range(K):
                    if n + k:
                        dve.wait_ge(bias_chain, n * K + k)
                    ins = nc.vector.scalar_tensor_tensor(
                        out=vrow[:], in0=bank[5][:, C * k:C * k + C], scalar=att[:, n, k:k + 1], in1=vrow[:],
                        op0=ALU.mult, op1=ALU.add).then_inc(bias_chain, 1)
                dve.wait_ge(bias_chain, n * K + K)
                if n < NL - 1:
                    nc.vector.tensor_copy(top[:, 0:1], vrow[:, 0:1]).then_inc(vrow_set, 1)
                else:
                    src = vrow[:].rearrange("b (g o i) -> b g o i", g=G, o=1)
                    nc.vector.tensor_copy(vdup[:], src.to_broadcast([B, G, 2, CG])).then_inc(vrow_set, 1)

            nc.vector.memset(mixtab[:, 0].bitcast(F32), 0.0).then_inc(mixtab_zero, 1)
            dve.wait_ge(toep_in, 16)
            taps = toep.rearrange("p (d g m) -> p d g m", d=2, g=G)
            eyes = eye_tap.rearrange("p (d o m) -> p d o m", d=2, o=1)
            nc.vector.tensor_tensor(taps, taps, eyes.to_broadcast([128, 2, G, 128]), ALU.add).then_inc(toep_set, 1)
            dve.wait_ge(c0_ps, 2)
            nc.vector.tensor_copy(vrow[:], bank[5][:, 0:C]).then_inc(c0_set, 1)
            dve.wait_ge(ones_set, 2)
            nc.vector.tensor_scalar(vcol[0:C, :], bank[6][0:C, 0:B], fcol, None, ALU.add).then_inc(c0_set, 1)
            dve.wait_ge(toep_hi_set, 1)
            nc.vector.tensor_tensor(toep_lo[:].rearrange("p d g m -> p (d g m)"), toep,
                                    toep_hi[:].rearrange("p d g m -> p (d g m)").bitcast(F32),
                                    ALU.subtract).then_inc(toep_lo_set, 1)
            dve.wait_ge(mats_hi_set, 1)
            nc.vector.tensor_tensor(mats_lo, mats, mats_hi.bitcast(F32),
                                    ALU.subtract).then_inc(mats_lo_set, 1)
            x_low(0, 0)
            logits = bank[4][:, 0:NL * K].rearrange("b (n k) -> b n k", n=NL)
            dve.wait_ge(logit_ps, 1)
            nc.vector.tensor_reduce(top[:], logits, AX_X, ALU.max).then_inc(softmax_chain, 1)
            dve.wait_ge(softmax_chain, 1)
            nc.vector.tensor_tensor(expo[:], logits, top[:].unsqueeze(2).to_broadcast([B, NL, K]),
                                    ALU.subtract).then_inc(centred, 1)
            dve.wait_ge(exp_set, 1)
            nc.vector.tensor_reduce(total[:], expo[:], AX_X, ALU.add).then_inc(softmax_chain, 1)
            dve.wait_ge(softmax_chain, 2)
            nc.vector.reciprocal(recip[:], total[:]).then_inc(softmax_chain, 1)
            dve.wait_ge(softmax_chain, 3)
            nc.vector.tensor_tensor(att[:], expo[:], recip[:].unsqueeze(2).to_broadcast([B, NL, K]),
                                    ALU.mult).then_inc(att_set, 1)
            dve.wait_ge(parts_zero, 2)
            dve.wait_ge(att_set, 1)
            twice = att[:].unsqueeze(2).to_broadcast([B, NL, 2, K])
            high = att_parts[:, :, 0::2, 0:K]
            nc.vector.tensor_copy(high, twice).then_inc(parts_set, 1)
            dve.wait_ge(parts_set, 1)
            nc.vector.tensor_tensor(att_parts[:, :, 1::2, 0:K], twice, high.bitcast(F32),
                                    ALU.subtract).then_inc(parts_set, 1)
            bias_sum(0)
            x_low(1, 1)

            def table_bank(t):
                n, c = divmod(t, TG)
                dve.wait_ge(tab_ps, t + 1)
                src = t_bank[t % 3][C:2 * C, :].rearrange("m (i p h) -> m p i h", i=NG, h=2)
                at = NH + NG * c
                for h in range(2):
                    last = nc.vector.tensor_copy(table[n][C * h:C * h + C, :, at:at + NG], src[:, :, :, h])
                last.then_inc(tab_dve, 1)

            t_bank = [bank[4], bank[6], bank[7]]
            for t in range(NTAB):
                if shared(t):
                    table_bank(t)
                if t == TG + 1:
                    x_low(2, 0)
                if t - 1 in BIAS_PRODUCTS:
                    bias_sum(BIAS_PRODUCTS.index(t - 1) + 1)
            y_high(0, 0, 0)
            y_low(0, 0)
            x_low(3, 1)
            mix_full(0)
            mix_low(0, 0)
            dve.wait_ge(vcol_set, NL)
            finish(0, 0, 0, 1)
            y_high(1, 0, 1)
            y_low(1, 1)
            mix_full(1)
            mix_low(1, 1)
            finish(0, 0, 0, 3)

            def step(q, it, par, it_prev):
                if not isinstance(q, int) or q + 1 < NQ:
                    x_low(q + 1, 1 - par)
                y_high(q - 1, it_prev, 1 - par)
                finish(q - 2, it - 1, par, 1)
                mix_full(q - 1)
                y_low(q - 1, 1 - par)
                mix_low(q - 1, 1 - par)
                finish(q - 2, it - 1, par, 3)

            step(3, 1, 1, 1)
            with dve.Fori(PEEL // 2, NQ // 2 - 1) as it:
                step(2 * it, it, 0, it - 1)
                step(2 * it + 1, it, 1, it)
            step(NQ - 2, NQ // 2 - 1, 0, NQ // 2 - 2)
            step(NQ - 1, NQ // 2 - 1, 1, NQ // 2 - 1)
            y_high(NQ - 1, NQ // 2 - 1, 1)
            mix_full(NQ - 1)
            y_low(NQ - 1, 1)
            mix_low(NQ - 1, 1)
            finish(NQ - 2, NQ // 2 - 1, 0, 1)
            finish(NQ - 2, NQ // 2 - 1, 0, 3)
            finish(NQ - 1, NQ // 2 - 1, 1, 1)
            finish(NQ - 1, NQ // 2 - 1, 1, 3)


def toeplitz(weight):
    w = weight.reshape(G, CG, CG, TAPS)
    out = np.zeros((CG, PH, 2, G, 2, CG, QP), weight.dtype)
    for p in range(PH):
        for n in range(PH):
            for d in range(2):
                tap = p + PH * d - n
                if 0 <= tap < TAPS:
                    out[:, p, d, :, n % 2, :, n // 2] = w[:, :, :, tap].transpose(2, 0, 1)
    return out.reshape(128, 2, G, 128)


def kernel(**inputs):
    import concourse.bacc as bacc
    from concourse.bass_utils import run_bass_kernel_spmd

    a = {k: np.asarray(v) for k, v in inputs.items()}
    f = np.float32
    mixes = [f"L{n}_cond_" for n in (1, 2, 3)]

    x = np.pad(a["x"], ((0, 0), (0, 0), (PAD, PH - PAD)))
    x = x.reshape(NQ, S, G, CG, JX, PH).transpose(0, 3, 5, 2, 1, 4).reshape(NQ * 128, G * S * JX)
    eye_tap = np.zeros((CG, PH, 2, 2, CG, QP), f)
    for c in range(CG):
        for n in range(PH):
            d, p = divmod(n + PAD, PH)
            eye_tap[c, p, d, n % 2, c, n // 2] = 1
    parity = np.zeros((G, 2, CG, 2), f)
    parity[:, 0, :, 0] = 1
    parity[:, 1, :, 1] = 1
    eye = np.eye(C, dtype=f)

    def table_rows(w, m_is_out):
        w = np.concatenate([w, eye[None]])
        w = w if m_is_out else w.transpose(0, 2, 1)
        return w.reshape(KR, C, 2, NH).transpose(0, 3, 2, 1)

    def pack(parts, widths):
        parts = [np.asarray(parts[n]).reshape(-1, w) for n, w in widths.items()]
        rows = max(len(p) for p in parts)
        return np.concatenate([np.pad(p, ((0, rows - len(p)), (0, 0))) for p in parts], 1)

    ws = [a[p + "weight"].reshape(K, C, C) for p in mixes]
    net = {
        "cond": a["cond_128"].T,
        "w0": np.stack([a[p + "W0"] for p in mixes], 1),
        "w1": np.stack([a[p + "W1"] for p in mixes], 1),
        "w2": np.stack([a[p + "W2"] for p in mixes], 1),
        "b01": np.stack([np.stack([a[p + b] for p in mixes], 1) for b in ("b0", "b1")], 1),
        "cw": a["L0_cond_c_weight"].T,
        "fcol": a["fside_S_0"],
    }
    biask = np.stack([a[p + "bias_k"].reshape(K * C) for p in mixes])
    arrays = {
        "x": x,
        "net": pack(net, NET),
        "kept": pack({"ident": np.eye(128, dtype=f), "parity": parity}, KEPT),
        "row": pack({"frow": a["fside_S_0"], "b2": np.concatenate([a[p + "b2"] for p in mixes])}, ROW),
        "toep": pack({"toep": toeplitz(a["L0_cond_weight"]), "eye_tap": eye_tap}, TOEP),
        "mixrow": np.concatenate([np.stack([w.transpose(2, 0, 1).reshape(C, K * C) for w in ws], 1),
                                  biask[None]]),
        "mats": np.stack([table_rows(w, n == 0) for n, w in enumerate(ws)], 1).reshape(KR * CH, CW),
    }
    nc = bacc.Bacc("TRN2", target_bir_lowering=False, num_devices=1)
    sent, args = {}, []
    for name, v in arrays.items():
        v = np.ascontiguousarray(v)
        sent[f"in_{name}"] = v
        args.append(nc.dram_tensor(f"in_{name}", v.shape, mybir.dt.from_np(v.dtype), kind="ExternalInput").ap())
    args.append(nc.dram_tensor("out", (NQ * 128, S * QP * J), F32, kind="ExternalOutput").ap())
    cond_resid_kernel(nc, *args)
    got = run_bass_kernel_spmd(nc, [sent], core_ids=[0]).results[0]["out"]
    return got.reshape(NQ, G, 2, CG, S, QP, J).transpose(0, 4, 1, 3, 6, 5, 2).reshape(B, C, L)
```

```python
from contextlib import ExitStack

import numpy as np

import concourse.bass as bass
from concourse import mybir

F32 = mybir.dt.float32
F32R = mybir.dt.float32r
ALU = mybir.AluOpType
ACT = mybir.ActivationFunctionType
AX_X = mybir.AxisListType.X

B, C, L = 128, 64, 1024
G, CG = 4, 16
TAPS, PAD = 9, 4
PH = 8
J = L // PH
QP = PH // 2
JX = J + 1
S = 4
NQ = B // S
PR = S // 2
D = 128
K = 8
KR = K + 1
PARTS = 3
NL = 3
N = S * J
NH = C // 2
NG = 4
TG = NH // NG
NTAB = NL * TG
BIAS_TURNS = (4, 12)
BIAS_PRODUCTS = (8, 15)
CONV_AFTER = {1: (0, 0), 2: (0, 1), 3: (0, 2), 4: (0, 3), 9: (1, 0), 11: (1, 1), 13: (1, 2), 14: (1, 3), 19: (2, 0), 22: (2, 1)}
SPLIT_AT = {0: 1, 9: 2, 18: 3}
POOL_LOW = (1,)
ACT_ALONE = (8, 10, 12, 20)
DVE_ALONE = (2, 3, 5, 9, 11)
YHIGH_AT = 19
CH = 12
CW = NL * NH * 2 * C // CH
NET = dict(cond=B, w0=NL * D, b01=2 * NL, cw=C, fcol=1, w1=NL * D, w2=NL * K)
FIRST = NET["cond"] + NET["w0"] + NET["b01"]
KEPT = dict(ident=128, parity=2)
ROW = dict(frow=C, b2=NL * K)
TOEP = dict(toep=2 * G * 128, eye_tap=2 * 128)


def columns(tile, widths):
    out, at = {}, 0
    for name, n in widths.items():
        out[name] = tile[:, at:at + n]
        at += n
    return out


def cond_resid_kernel(nc, x_h, net_h, kept_h, row_h, toep_h, mixrow_h, mats_h, out_h):
    with ExitStack() as ctx:
        def sb(name, shape, dt=F32):
            return ctx.enter_context(nc.sbuf_tensor(name, shape, dt))

        def sem(name):
            return ctx.enter_context(nc.semaphore(name))

        bank = [ctx.enter_context(nc.psum_tensor(f"bank{i}", [128, 512], F32)) for i in range(8)]
        conv_ps, mix_ps = bank[0:4], bank[4:6]
        pair_ps, comp_ps = bank[6], bank[7]
        hid1_bank, hid2_bank = (bank[4], bank[6], bank[7]), bank[1:4]
        t_bank = (bank[4], bank[6], bank[7], bank[2], bank[3])
        TB = len(t_bank)

        table = [sb(f"table{n}", [128, B // 2, C]) for n in range(NL)]
        early = columns(table[2][:].rearrange("p b c -> p (b c)"), dict(net=sum(NET.values()), mixrow=NL * K * C))
        net = early["net"]
        mixrow = early["mixrow"][0:C + 1].rearrange("p (n m) -> p n m", n=NL)
        kept = sb("kept", [128, sum(KEPT.values())])
        row = sb("row", [1, sum(ROW.values())])
        part = columns(net, NET)
        cond, cw = part["cond"], part["cw"]
        ident, parity = columns(kept, KEPT).values()
        w0, w1, w2 = (part[n].rearrange("p (n m) -> p n m", n=NL) for n in ("w0", "w1", "w2"))
        b01 = part["b01"].rearrange("p (t n) -> p t n", t=2)
        fcol = part["fcol"][0:C, :]
        frow, b2 = columns(row, ROW).values()
        toep_hi = sb("toep_hi", [128, 2, G, 128], F32R)
        toep_lo = sb("toep_lo", [128, 2, G, 128], F32R)
        mixtab = sb("mixtab", [128, NL, NH, 2 * C], F32R)
        ones = sb("ones", [1, B])
        top = sb("top", [B, NL])
        expo = sb("expo", [B, NL, K])
        total = sb("total", [B, NL])
        recip = sb("recip", [B, NL])
        att = sb("att", [B, NL, K])
        att_pad = sb("att_pad", [B, NL, 128], F32R)
        att_parts = att_pad[:, :, 0:PARTS * KR].rearrange("b n (t k) -> b n t k", t=PARTS)
        att_t = sb("att_t", [128, NL, B], F32R)
        vrow = sb("vrow", [B, C])
        vcol = sb("vcol", [C + 1, B])
        vdup = sb("vdup", [B, G, 2, CG])
        beta = sb("beta", [128, B])

        x_sb = sb("x_sb", [128, 2, G, S, JX])
        x_hi = sb("x_hi", [128, 2, G, S, JX], F32R)
        x_lo = sb("x_lo", [128, 2, G, S, JX], F32R)
        conv_sb = sb("conv_sb", [128, 2, G, N])
        out_sb = sb("out_sb", [128, 2, S, QP * J])
        y_sb, y_hi, y_lo = (mixtab[:, n].rearrange("p (r h s) j -> p r h s j", r=2, h=QP) for n in range(NL))
        y_sb = y_sb.bitcast(F32)
        mats = x_sb[:, 1].rearrange("p g s j -> p (g s j)")[0:KR * CH, 0:CW]
        mats_hi = conv_sb[:, 1].rearrange("p g n -> p (g n)")[0:KR * CH, 0:CW].bitcast(F32R)
        mats_lo = out_sb[:, 0].rearrange("p s n -> p (s n)")[0:KR * CH, 0:CW].bitcast(F32R)
        vadd = out_sb[:, 0].rearrange("p s n -> p (s n)")[:, CW:CW + C]
        second = columns(out_sb[:, 1].rearrange("p s n -> p (s n)"), dict(TOEP, hid1=NL * B, hid2=NL * B))
        toep, eye_tap = second["toep"], second["eye_tap"]
        toep_all = out_sb[:, 1].rearrange("p s n -> p (s n)")[:, 0:sum(TOEP.values())]
        hid1, hid2 = (second[n].rearrange("p (n b) -> p n b", n=NL) for n in ("hid1", "hid2"))
        a1_pair = sb("a1_pair", [128, 2, PR, C])
        a2_diag = sb("a2_diag", [128, 2, PR, 2 * C])
        a3_diag = sb("a3_diag", [128, 2, PR, 2 * C])
        a21_dup = sb("a21_dup", [128, 2, PR, G, 2, CG])
        mix_f = sb("mix_f", [128, S * G, 2, CG])
        mix_hi = sb("mix_hi", [128, 2, S, 128], F32R)
        mix_lo = sb("mix_lo", [128, 2, S, 128], F32R)

        net0_in, net_in, kept_in, toep_in, mats_in, mixrow_in, tab_in = (
            sem(n) for n in ("net0_in", "net_in", "kept_in", "toep_in", "mats_in", "mixrow_in", "tab_in"))
        mats_hi_set, mats_lo_set, parts_zero, parts_set = (
            sem(n) for n in ("mats_hi_set", "mats_lo_set", "parts_zero", "parts_set"))
        mixtab_zero = sem("mixtab_zero")
        x_in = [sem("x_in0"), sem("x_in1")]
        stored = [sem("stored0"), sem("stored1")]
        ones_set, toep_set, zeros_set = sem("ones_set"), sem("toep_set"), sem("zeros_set")
        hid1_ps, hid1_set, hid2_ps, hid2_set = sem("hid1_ps"), sem("hid1_set"), sem("hid2_ps"), sem("hid2_set")
        c0_ps, c0_set = sem("c0_ps"), sem("c0_set")
        logit_ps, centred, exp_set, att_set = sem("logit_ps"), sem("centred"), sem("exp_set"), sem("att_set")
        softmax_chain, bias_chain = sem("softmax_chain"), sem("bias_chain")
        att_t_ps, att_t_set = sem("att_t_ps"), sem("att_t_set")
        prod_ps, vrow_set, vcol_ps, vcol_set = sem("prod_ps"), sem("vrow_set"), sem("vcol_ps"), sem("vcol_set")
        tab_ps, tab_act, tab_dve = sem("tab_ps"), sem("tab_act"), sem("tab_dve")
        toep_hi_set, toep_lo_set = sem("toep_hi_set"), sem("toep_lo_set")
        xhi_set, xlo_set, conv_done, conv_out = (sem(n) for n in ("xhi_set", "xlo_set", "conv_done", "conv_out"))
        moved = [sem("moved0"), sem("moved1")]
        yhi_set, ylo_set, a3_in = sem("yhi_set"), sem("ylo_set"), sem("a3_in")
        pair_in, a21_ps, a21_set, comp_done = sem("pair_in"), sem("a21_ps"), sem("a21_set"), sem("comp_done")
        mixf_set, mixhi_set, mixlo_set = sem("mixf_set"), sem("mixhi_set"), sem("mixlo_set")
        mix_done, out_act, out_dve = sem("mix_done"), sem("out_act"), sem("out_dve")

        def act_halves(t):
            return () if t in DVE_ALONE else (0, 1) if t in ACT_ALONE else (0,)

        def dve_halves(t):
            return () if t in ACT_ALONE else (0, 1) if t in DVE_ALONE else (1,)

        def act_banks(t):
            return sum(bool(act_halves(u)) for u in range(t))

        def dve_banks(t):
            return sum(bool(dve_halves(u)) for u in range(t))

        PEEL = 4

        def wait(eng, s, value):
            if not isinstance(value, int) or value > 0:
                eng.wait_ge(s, value)

        block = ctx.enter_context(nc.Block())

        @block.sync
        def _(sp):
            def load(q, par):
                sp.dma_start(x_sb[:, par].rearrange("p g s j -> p (g s j)"),
                             x_h[bass.ds(q * 128, 128), :]).then_inc(x_in[par], 16)

            def store(q, par):
                sp.wait_ge(out_dve, q + 1)
                sp.wait_ge(out_act, 3 * q + 3)
                sp.dma_start(out_h[bass.ds(q * 128, 128), :],
                             out_sb[:, par].rearrange("p s n -> p (s n)")).then_inc(stored[par], 16)

            def move(q, par, g):
                if g == 0:
                    wait(sp, ylo_set, q - 1)
                sp.wait_ge(conv_out, 4 * q + g + 1)
                sp.dma_start(y_sb[32 * g:32 * g + 32, par].rearrange("p h s j -> p h (s j)"),
                             conv_sb[:, par, g, :]).then_inc(moved[par], 16)

            sp.dma_start(net[:, 0:FIRST], net_h[:, 0:FIRST]).then_inc(net0_in, 16)
            sp.dma_start(net[:, FIRST:], net_h[:, FIRST:]).then_inc(net_in, 16)
            sp.dma_start(row[:], row_h).then_inc(net_in, 16)
            sp.dma_start(mats, mats_h).then_inc(mats_in, 16)
            sp.dma_start(toep_all, toep_h).then_inc(toep_in, 16)
            sp.dma_start(kept[:], kept_h).then_inc(kept_in, 16)
            load(0, 0)
            sp.dma_start(mixrow, mixrow_h).then_inc(mixrow_in, 16)
            sp.wait_ge(mixtab_zero, 2)
            for i, (src, ready) in enumerate(((mats_hi, mats_hi_set), (mats_hi, mats_hi_set), (mats_lo, mats_lo_set))):
                sp.wait_ge(ready, 1)
                dst = mixtab[KR * i:KR * i + KR].rearrange("k n c m -> k (n c m)").rearrange("k (c n) -> k c n", c=CH)
                sp.dma_start(dst.bitcast(F32), src.bitcast(F32)).then_inc(tab_in, 16)
            load(1, 1)
            sp.wait_ge(xhi_set, 1)
            sp.wait_ge(xlo_set, 1)
            load(2, 0)
            sp.wait_ge(tab_ps, TG)
            for g in range(G):
                move(0, 0, g)

            def step(q, par):
                if not isinstance(q, int) or q + 2 < NQ:
                    sp.wait_ge(xhi_set, q + 1)
                    sp.wait_ge(xlo_set, q + 1)
                    load(q + 2, par)
                move(q, par, 0)
                if not isinstance(q, int) or q >= 3:
                    store(q - 3, 1 - par)
                for g in range(1, G):
                    move(q, par, g)

            for q in range(1, PEEL):
                step(q, q % 2)
            with sp.Fori(PEEL // 2, NQ // 2 - 1) as it:
                step(2 * it, 0)
                step(2 * it + 1, 1)
            step(NQ - 2, 0)
            step(NQ - 1, 1)
            for q in range(NQ - 3, NQ - 1):
                store(q, q % 2)
            for h in range(2):
                sp.wait_ge(out_act, 3 * (NQ - 1) + h + 1)
                sp.wait_ge(out_dve, NQ + h)
                rows = slice((NQ - 1) * 128, NQ * 128)
                sp.dma_start(out_h[rows, h * 2 * QP * J:(h + 1) * 2 * QP * J],
                             out_sb[:, 1, 2 * h:2 * h + 2].rearrange("p s n -> p (s n)")).then_inc(stored[1], 16)
            sp.wait_ge(stored[0], 16 * (NQ // 2))
            sp.wait_ge(stored[1], 16 * (NQ // 2 + 1))

        @block.gpsimd
        def _(pool):
            nc.gpsimd.memset(ones[:], 1.0).then_inc(ones_set, 1)
            nc.gpsimd.memset(vcol[:], 1.0).then_inc(ones_set, 1)
            nc.gpsimd.memset(mixtab[:, 1:].bitcast(F32), 0.0).then_inc(mixtab_zero, 1)
            nc.gpsimd.memset(att_pad[:].bitcast(F32), 0.0).then_inc(parts_zero, 1)
            pool.wait_ge(parts_zero, 1)
            nc.gpsimd.memset(att_parts[:, :, 0::2, K:KR].bitcast(F32), 1.0).then_inc(parts_zero, 1)
            nc.gpsimd.memset(a2_diag[:], 0.0).then_inc(zeros_set, 1)
            nc.gpsimd.memset(a3_diag[:], 0.0).then_inc(zeros_set, 1)
            pool.wait_ge(zeros_set, 2)

            def lower_mats(q, par):
                wait(pool, a21_ps, q - 1)
                wait(pool, a3_in, 2 * q if not isinstance(q, int) or q > 1 else 0)
                here = bass.ds(PR * q, PR)
                wait(pool, pair_in, 3 * q)
                nc.gpsimd.tensor_copy(a1_pair[:, par], table[0][:, here, :]).then_inc(pair_in, 1)
                for h in range(2):
                    rows = slice(C * h, C * h + C)
                    pool.wait_ge(pair_in, 3 * q + h + 1)
                    nc.gpsimd.tensor_copy(a2_diag[rows, par, :, C * h:C * h + C],
                                          table[1][rows, here, :]).then_inc(pair_in, 1)

            def upper_mats(q, par):
                wait(pool, comp_done, q - 1)
                pool.wait_ge(pair_in, 3 * q + 3)
                here = bass.ds(PR * q, PR)
                for h in range(2):
                    rows = slice(C * h, C * h + C)
                    wait(pool, a3_in, 2 * q + h)
                    nc.gpsimd.tensor_copy(a3_diag[rows, par, :, C * h:C * h + C],
                                          table[2][rows, here, :]).then_inc(a3_in, 1)

            def tables_full(t):
                pool.wait_ge(tab_act, act_banks(t))
                pool.wait_ge(tab_dve, dve_banks(t))

            for q in POOL_LOW:
                par = q % 2
                pool.wait_ge(xhi_set, q + 1)
                wait(pool, conv_done, 4 * q - 4)
                pool.wait_ge(xlo_set, q)
                nc.gpsimd.tensor_tensor(x_lo[:, par].rearrange("p g s j -> p (g s j)"),
                                        x_sb[:, par].rearrange("p g s j -> p (g s j)"),
                                        x_hi[:, par].rearrange("p g s j -> p (g s j)").bitcast(F32),
                                        ALU.subtract).then_inc(xlo_set, 1)

            tables_full(2 * TG)
            lower_mats(0, 0)
            lower_mats(1, 1)
            pool.wait_ge(pair_in, 6)
            tables_full(NTAB)
            upper_mats(0, 0)
            upper_mats(1, 1)

            def step(q, par):
                lower_mats(q, par)
                upper_mats(q, par)

            for q in range(2, PEEL):
                step(q, q % 2)
            with pool.Fori(PEEL // 2, NQ // 2) as it:
                step(2 * it, 0)
                step(2 * it + 1, 1)

        @block.tensor
        def _(pe):
            mm = nc.tensor.matmul

            def conv(q, par, g, banks=G):
                if g == 0:
                    pe.wait_ge(xhi_set, q + 1)
                    pe.wait_ge(xlo_set, q + 1)
                wait(pe, conv_out, 4 * q + g + 1 - banks)
                o = conv_ps[g % banks][:, :].rearrange("p (s j) -> p s j", s=S)
                for i, (w, v) in enumerate(((toep_hi, x_hi), (toep_lo, x_hi), (toep_hi, x_lo))):
                    for d in range(2):
                        last = mm(o, w[:, d, g, :], v[:, par, g, :, d:d + J], start=i + d == 0, stop=i + d == 3)
                last.then_inc(conv_done, 1)

            def compose_lower(q, par):
                pe.wait_ge(pair_in, 3 * q + 3)
                wait(pe, a21_set, 2 * q)
                for pr in range(PR):
                    last = mm(pair_ps[:, C * pr:C * pr + C], a2_diag[:, par, pr, :], a1_pair[:, par, pr, :],
                              start=True, stop=True)
                last.then_inc(a21_ps, 1)

            def compose_upper(q, par):
                pe.wait_ge(a21_set, 2 * q + 2)
                pe.wait_ge(a3_in, 2 * q + 2)
                wait(pe, mixf_set, 2 * q)
                for pr in range(PR):
                    last = mm(comp_ps[:, 128 * pr:128 * pr + 128],
                              a21_dup[:, par, pr].rearrange("p g r i -> p (g r i)"), a3_diag[:, par, pr, :],
                              start=True, stop=True)
                last.then_inc(comp_done, 1)

            def mix(q, par, s):
                if s == 0:
                    pe.wait_ge(yhi_set, q + 1)
                    pe.wait_ge(ylo_set, q + 1)
                    pe.wait_ge(mixlo_set, q + 1)
                if isinstance(q, int) and q == NQ - 1 and s == S // 2:
                    pe.wait_ge(yhi_set, NQ + 1)
                    pe.wait_ge(ylo_set, NQ + 1)
                if s == 3:
                    pe.wait_ge(out_dve, q + 1)
                else:
                    wait(pe, out_act, 3 * q + s - 1)
                m_hi, m_lo = mix_hi[:, par, s, :], mix_lo[:, par, s, :]
                v_hi, v_lo = y_hi[:, par, :, s, :], y_lo[:, par, :, s, :]
                o = mix_ps[s % 2][:, :].rearrange("p (h j) -> p h j", h=QP)
                mm(o, m_hi, v_hi, start=True, stop=False)
                mm(o, m_lo, v_hi, start=False, stop=False)
                mm(o, m_hi, v_lo, start=False, stop=True).then_inc(mix_done, 1)

            pe.wait_ge(net0_in, 16)
            for n in range(NL):
                mm(hid1_bank[n][:, 0:B], w0[:, n, :], cond, start=True, stop=True).then_inc(hid1_ps, 1)
            pe.wait_ge(net_in, 32)
            for n in range(NL):
                pe.wait_ge(hid1_set, n + 1)
                mm(hid2_bank[n][:, 0:B], w1[:, n, :], hid1[:, n, :], start=True, stop=True).then_inc(hid2_ps, 1)
            pe.wait_ge(ones_set, 2)
            logits = bank[4][:, 0:NL * K]
            mm(logits, ones[:], b2, start=True, stop=False)
            for n in range(NL):
                pe.wait_ge(hid2_set, n + 1)
                mm(logits[:, K * n:K * n + K], hid2[:, n, :], w2[:, n, :], start=False,
                   stop=n == NL - 1).then_inc(logit_ps, 1)
            mm(bank[5][:, 0:C], cond, cw, start=True, stop=False)
            mm(bank[5][:, 0:C], ones[:], frow, start=False, stop=True).then_inc(c0_ps, 1)
            mm(bank[6][0:C, 0:B], cw, cond, start=True, stop=True).then_inc(c0_ps, 1)

            def bias_products(n):
                if n == 0:
                    pe.wait_ge(mixrow_in, 16)
                    pe.wait_ge(c0_set, 2)
                else:
                    pe.wait_ge(vcol_set, n)
                mm(bank[5][:, :], vcol[:], mixrow[:, n, :], start=True, stop=True).then_inc(prod_ps, 1)

            def bias_turn(n):
                pe.wait_ge(vrow_set, n + 1)
                nc.tensor.transpose(bank[5][0:C, 0:B], vrow[:], ident).then_inc(vcol_ps, 1)

            pe.wait_ge(parts_set, 2)
            pe.wait_ge(kept_in, 16)
            for n in range(NL):
                last = nc.tensor.transpose(bank[7][:, B * n:B * n + B], att_pad[:, n, :].bitcast(F32), ident)
            last.then_inc(att_t_ps, 1)
            bias_products(0)
            pe.wait_ge(toep_hi_set, 1)
            pe.wait_ge(toep_lo_set, 1)
            pe.wait_ge(att_t_set, 1)
            pe.wait_ge(tab_in, 16 * PARTS)
            pe.wait_ge(c0_set, 2)
            for t in range(NTAB):
                n, c = divmod(t, TG)
                if t >= TB:
                    pe.wait_ge(tab_act, act_banks(t - TB + 1))
                    pe.wait_ge(tab_dve, dve_banks(t - TB + 1))
                for i in range(NG):
                    last = mm(t_bank[t % TB][:, B * i:B * i + B], mixtab[:, n, NG * c + i, :], att_t[:, n, :],
                              start=True, stop=True)
                last.then_inc(tab_ps, 1)
                if t in CONV_AFTER:
                    q, g = CONV_AFTER[t]
                    conv(q, q % 2, g, banks=2)
                if t in BIAS_PRODUCTS:
                    bias_products(BIAS_PRODUCTS.index(t) + 1)
                if t in BIAS_TURNS:
                    bias_turn(BIAS_TURNS.index(t))
            pe.wait_ge(vrow_set, NL)
            nc.tensor.transpose(bank[5][:, 0:B], vdup[:].rearrange("b g r o -> b (g r o)"),
                                ident).then_inc(vcol_ps, 1)
            conv(2, 0, 2, banks=2)
            pe.wait_ge(tab_act, act_banks(NTAB))
            pe.wait_ge(tab_dve, dve_banks(NTAB))
            compose_lower(0, 0)
            conv(2, 0, 3, banks=2)
            compose_upper(0, 0)
            compose_lower(1, 1)
            pe.wait_ge(conv_out, 12)
            conv(3, 1, 0)
            mix(0, 0, 0)
            pe.wait_ge(vcol_set, NL)
            mix(0, 0, 1)
            compose_upper(1, 1)
            mix(0, 0, 2)
            mix(0, 0, 3)
            conv(3, 1, 1)

            def step(q, par, done=0):
                for g in range(G):
                    if g >= done:
                        conv(q, par, g)
                    if g == 0:
                        compose_lower(q - 1, 1 - par)
                    mix(q - 2, par, g)
                    if g == 1:
                        compose_upper(q - 1, 1 - par)

            step(3, 1, done=2)
            with pe.Fori(PEEL // 2, NQ // 2) as it:
                step(2 * it, 0)
                step(2 * it + 1, 1)
            compose_lower(NQ - 1, 1)
            for s in range(S // 2):
                mix(NQ - 2, 0, s)
            compose_upper(NQ - 1, 1)
            for s in range(S // 2, S):
                mix(NQ - 2, 0, s)
            for s in range(S):
                mix(NQ - 1, 1, s)

        @block.scalar
        def _(act):
            def x_high(q, it, par):
                act.wait_ge(x_in[par], 16 * it + 16)
                wait(act, conv_done, 4 * q - 4)
                nc.scalar.activation(x_hi[:, par].rearrange("p g s j -> p (g s j)"),
                                     x_sb[:, par].rearrange("p g s j -> p (g s j)"), ACT.Copy).then_inc(xhi_set, 1)

            def conv_copy(q, it, par, g, banks=G):
                act.wait_ge(conv_done, 4 * q + g + 1)
                if g == 0:
                    wait(act, moved[par], 16 * G * it)
                nc.scalar.activation(conv_sb[:, par, g, :], conv_ps[g % banks][:, :], ACT.Copy).then_inc(conv_out, 1)

            def y_high(q, it, par):
                act.wait_ge(moved[par], 16 * G * it + 16 * G)
                act.wait_ge(tab_ps, 2 * TG)
                nc.scalar.activation(y_hi[:, par].rearrange("p h s j -> p (h s j)"),
                                     y_sb[:, par].rearrange("p h s j -> p (h s j)"), ACT.Copy).then_inc(yhi_set, 1)

            def a21_copy(q, par):
                act.wait_ge(a21_ps, q + 1)
                wait(act, comp_done, q - 1)
                for pr in range(PR):
                    src = pair_ps[:, C * pr:C * pr + C].rearrange("p (g o i) -> p g o i", g=G, o=1)
                    nc.scalar.activation(a21_dup[:, par, pr], src.to_broadcast([128, G, 2, CG]),
                                         ACT.Copy).then_inc(a21_set, 1)

            def mix_high(q, par):
                act.wait_ge(mixf_set, 2 * q + 2)
                nc.scalar.activation(mix_hi[:, par].rearrange("p s n -> p (s n)"),
                                     mix_f[:].rearrange("p a r o -> p (a r o)"), ACT.Copy).then_inc(mixhi_set, 1)

            def finish(q, it, par, s):
                act.wait_ge(mix_done, 4 * q + s + 1)
                if s == 0:
                    wait(act, stored[par], 16 * it)
                nc.scalar.activation(out_sb[:, par, s, :], mix_ps[s % 2][:, :], ACT.Identity,
                                     bias=beta[:, bass.ds(S * q + s, 1)]).then_inc(out_act, 1)

            for n in range(NL):
                act.wait_ge(hid1_ps, n + 1)
                if n == 0:
                    act.wait_ge(net0_in, 16)
                nc.scalar.activation(hid1[:, n, :], hid1_bank[n][:, 0:B], ACT.Gelu,
                                     bias=b01[:, 0, n:n + 1]).then_inc(hid1_set, 1)
            for n in range(NL):
                act.wait_ge(hid2_ps, n + 1)
                nc.scalar.activation(hid2[:, n, :], hid2_bank[n][:, 0:B], ACT.Gelu,
                                     bias=b01[:, 1, n:n + 1]).then_inc(hid2_set, 1)
            act.wait_ge(toep_set, 1)
            nc.scalar.activation(toep_hi[:].rearrange("p d g m -> p (d g m)"), toep,
                                 ACT.Copy).then_inc(toep_hi_set, 1)
            act.wait_ge(centred, 1)
            nc.scalar.activation(expo[:], expo[:], ACT.Exp).then_inc(exp_set, 1)
            x_high(0, 0, 0)
            act.wait_ge(att_t_ps, 1)
            nc.scalar.activation(att_t[:], bank[7][:, 0:NL * B].rearrange("k (n b) -> k n b", n=NL),
                                 ACT.Copy).then_inc(att_t_set, 1)

            def table_bank(t):
                n, c = divmod(t, TG)
                act.wait_ge(tab_ps, t + 1)
                for half in act_halves(t):
                    src = t_bank[t % TB][C * half:C * half + C, :].rearrange("m (i p h) -> m p i h", i=NG, h=2)
                    at = NH * half + NG * c
                    for h in range(2):
                        last = nc.scalar.activation(table[n][C * h:C * h + C, :, at:at + NG],
                                                    src[:, :, :, h], ACT.Copy)
                    if half == act_halves(t)[-1]:
                        last.then_inc(tab_act, 1)

            for t in range(NTAB):
                table_bank(t)
                if t - 1 in CONV_AFTER:
                    q, g = CONV_AFTER[t - 1]
                    conv_copy(q, q // 2, q % 2, g, banks=2)
                if t == YHIGH_AT:
                    y_high(0, 0, 0)
                if t in SPLIT_AT:
                    q = SPLIT_AT[t]
                    x_high(q, q // 2, q % 2)
                if t - 1 in BIAS_TURNS:
                    act.wait_ge(vcol_ps, BIAS_TURNS.index(t - 1) + 1)
                    nc.scalar.activation(vcol[0:C, :], bank[5][0:C, 0:B], ACT.Copy).then_inc(vcol_set, 1)
            conv_copy(2, 1, 0, 2, banks=2)
            a21_copy(0, 0)
            y_high(1, 0, 1)
            conv_copy(2, 1, 0, 3, banks=2)
            act.wait_ge(vcol_ps, NL)
            nc.scalar.activation(beta[:], bank[5][:, 0:B], ACT.Copy).then_inc(vcol_set, 1)
            a21_copy(1, 1)
            mix_high(0, 0)
            conv_copy(3, 1, 1, 0)
            act.wait_ge(vcol_set, NL)
            finish(0, 0, 0, 0)
            x_high(4, 2, 0)
            mix_high(1, 1)
            finish(0, 0, 0, 2)

            def step(q, it, par, it_next, done=0):
                if not done and (not isinstance(q, int) or q + 1 < NQ):
                    x_high(q + 1, it_next, 1 - par)
                finish(q - 3, 0, 1 - par, 3)
                if not done:
                    conv_copy(q, it, par, 0)
                a21_copy(q - 1, 1 - par)
                finish(q - 2, it - 1, par, 0)
                conv_copy(q, it, par, 1)
                conv_copy(q, it, par, 2)
                mix_high(q - 1, 1 - par)
                finish(q - 2, it - 1, par, 2)
                conv_copy(q, it, par, 3)

            step(3, 1, 1, 2, done=1)
            with act.Fori(PEEL // 2, NQ // 2 - 1) as it:
                step(2 * it, it, 0, it)
                step(2 * it + 1, it, 1, it + 1)
            step(NQ - 2, NQ // 2 - 1, 0, NQ // 2 - 1)
            step(NQ - 1, NQ // 2 - 1, 1, NQ // 2)
            finish(NQ - 3, 0, 1, 3)
            a21_copy(NQ - 1, 1)
            finish(NQ - 2, NQ // 2 - 1, 0, 0)
            mix_high(NQ - 1, 1)
            act.wait_ge(moved[1], 16 * G * (NQ // 2))
            act.wait_ge(mix_done, 4 * (NQ - 2))
            for h in range(2):
                nc.scalar.activation(y_hi[:, 1, :, 2 * h:2 * h + 2, :], y_sb[:, 1, :, 2 * h:2 * h + 2, :],
                                     ACT.Copy).then_inc(yhi_set, 1)
            finish(NQ - 2, NQ // 2 - 1, 0, 2)
            finish(NQ - 2, NQ // 2 - 1, 0, 3)
            finish(NQ - 1, NQ // 2 - 1, 1, 0)
            finish(NQ - 1, NQ // 2 - 1, 1, 2)

        @block.vector
        def _(dve):
            def x_low(q, par):
                dve.wait_ge(xhi_set, q + 1)
                wait(dve, conv_done, 4 * q - 4)
                nc.vector.tensor_tensor(x_lo[:, par].rearrange("p g s j -> p (g s j)"),
                                        x_sb[:, par].rearrange("p g s j -> p (g s j)"),
                                        x_hi[:, par].rearrange("p g s j -> p (g s j)").bitcast(F32),
                                        ALU.subtract).then_inc(xlo_set, 1)

            def y_high(q, it, par):
                dve.wait_ge(moved[par], 16 * G * it + 16 * G)
                wait(dve, mix_done, 4 * q - 4)
                v, hi = (t[:, par].rearrange("p h s j -> p (h s j)") for t in (y_sb, y_hi))
                nc.vector.tensor_copy(hi, v).then_inc(yhi_set, 1)

            def y_low(q, par):
                dve.wait_ge(yhi_set, q + 1)
                v, hi, lo = (t[:, par].rearrange("p h s j -> p (h s j)") for t in (y_sb, y_hi, y_lo))
                nc.vector.tensor_tensor(lo, v, hi.bitcast(F32), ALU.subtract).then_inc(ylo_set, 1)

            def mix_full(q):
                dve.wait_ge(comp_done, q + 1)
                src = comp_ps[:, 0:S * C].rearrange("p (a o) -> p a o", o=CG)
                for r in range(2):
                    nc.vector.tensor_scalar(mix_f[:, :, r, :], src, parity[:, r:r + 1], None,
                                            ALU.mult).then_inc(mixf_set, 1)

            def mix_low(q, par):
                dve.wait_ge(mixhi_set, q + 1)
                nc.vector.tensor_tensor(mix_lo[:, par].rearrange("p s n -> p (s n)"),
                                        mix_f[:].rearrange("p a r o -> p (a r o)"),
                                        mix_hi[:, par].rearrange("p s n -> p (s n)").bitcast(F32),
                                        ALU.subtract).then_inc(mixlo_set, 1)

            def finish(q, it, par, s):
                dve.wait_ge(mix_done, 4 * q + s + 1)
                if s == 1:
                    wait(dve, stored[par], 16 * it)
                nc.vector.tensor_scalar(out_sb[:, par, s, :], mix_ps[s % 2][:, :],
                                        beta[:, bass.ds(S * q + s, 1)], None, ALU.add).then_inc(out_dve, 1)

            def bias_sum(n):
                dve.wait_ge(prod_ps, n + 1)
                if n == 0:
                    dve.wait_ge(c0_set, 2)
                terms = mix_f[:].rearrange("b g r i -> b (g r i)").rearrange("b (k c) -> b k c", k=K)
                nc.vector.tensor_tensor(terms, bank[5][:, :].rearrange("b (k c) -> b k c", k=K),
                                        att[:, n, :].unsqueeze(2).to_broadcast([B, K, C]),
                                        ALU.mult).then_inc(bias_chain, 1)
                dve.wait_ge(bias_chain, 3 * n + 1)
                nc.vector.tensor_reduce(vadd, terms.rearrange("b k c -> b c k"), AX_X,
                                        ALU.add).then_inc(bias_chain, 1)
                dve.wait_ge(bias_chain, 3 * n + 2)
                nc.vector.tensor_tensor(vrow[:], vrow[:], vadd, ALU.add).then_inc(bias_chain, 1)
                dve.wait_ge(bias_chain, 3 * n + 3)
                if n < NL - 1:
                    nc.vector.tensor_copy(top[:, 0:1], vrow[:, 0:1]).then_inc(vrow_set, 1)
                else:
                    src = vrow[:].rearrange("b (g o i) -> b g o i", g=G, o=1)
                    nc.vector.tensor_copy(vdup[:], src.to_broadcast([B, G, 2, CG])).then_inc(vrow_set, 1)

            nc.vector.memset(mixtab[:, 0].bitcast(F32), 0.0).then_inc(mixtab_zero, 1)
            dve.wait_ge(mats_in, 16)
            nc.vector.tensor_copy(mats_hi, mats).then_inc(mats_hi_set, 1)
            dve.wait_ge(mats_hi_set, 1)
            nc.vector.tensor_tensor(mats_lo, mats, mats_hi.bitcast(F32), ALU.subtract).then_inc(mats_lo_set, 1)
            dve.wait_ge(toep_in, 16)
            taps = toep.rearrange("p (d g m) -> p d g m", d=2, g=G)
            eyes = eye_tap.rearrange("p (d o m) -> p d o m", d=2, o=1)
            nc.vector.tensor_tensor(taps, taps, eyes.to_broadcast([128, 2, G, 128]), ALU.add).then_inc(toep_set, 1)
            logits = bank[4][:, 0:NL * K].rearrange("b (n k) -> b n k", n=NL)
            dve.wait_ge(logit_ps, NL)
            nc.vector.tensor_reduce(top[:], logits, AX_X, ALU.max).then_inc(softmax_chain, 1)
            dve.wait_ge(softmax_chain, 1)
            nc.vector.tensor_tensor(expo[:], logits, top[:].unsqueeze(2).to_broadcast([B, NL, K]),
                                    ALU.subtract).then_inc(centred, 1)
            dve.wait_ge(toep_hi_set, 1)
            nc.vector.tensor_tensor(toep_lo[:].rearrange("p d g m -> p (d g m)"), toep,
                                    toep_hi[:].rearrange("p d g m -> p (d g m)").bitcast(F32),
                                    ALU.subtract).then_inc(toep_lo_set, 1)
            dve.wait_ge(exp_set, 1)
            nc.vector.tensor_reduce(total[:], expo[:], AX_X, ALU.add).then_inc(softmax_chain, 1)
            dve.wait_ge(softmax_chain, 2)
            nc.vector.reciprocal(recip[:], total[:]).then_inc(softmax_chain, 1)
            dve.wait_ge(softmax_chain, 3)
            nc.vector.tensor_tensor(att[:], expo[:], recip[:].unsqueeze(2).to_broadcast([B, NL, K]),
                                    ALU.mult).then_inc(att_set, 1)
            dve.wait_ge(parts_zero, 2)
            dve.wait_ge(att_set, 1)
            twice = att[:].unsqueeze(2).to_broadcast([B, NL, 2, K])
            high = att_parts[:, :, 0::2, 0:K]
            nc.vector.tensor_copy(high, twice).then_inc(parts_set, 1)
            dve.wait_ge(parts_set, 1)
            nc.vector.tensor_tensor(att_parts[:, :, 1, 0:K], att[:], high[:, :, 0, :].bitcast(F32),
                                    ALU.subtract).then_inc(parts_set, 1)
            dve.wait_ge(c0_ps, 2)
            nc.vector.tensor_copy(vrow[:], bank[5][:, 0:C]).then_inc(c0_set, 1)
            dve.wait_ge(ones_set, 2)
            nc.vector.tensor_scalar(vcol[0:C, :], bank[6][0:C, 0:B], fcol, None, ALU.add).then_inc(c0_set, 1)
            x_low(0, 0)
            bias_sum(0)

            def table_bank(t):
                n, c = divmod(t, TG)
                dve.wait_ge(tab_ps, t + 1)
                for half in dve_halves(t):
                    src = t_bank[t % TB][C * half:C * half + C, :].rearrange("m (i p h) -> m p i h", i=NG, h=2)
                    at = NH * half + NG * c
                    for h in range(2):
                        last = nc.vector.tensor_copy(table[n][C * h:C * h + C, :, at:at + NG], src[:, :, :, h])
                    if half == dve_halves(t)[-1]:
                        last.then_inc(tab_dve, 1)

            for t in range(NTAB):
                table_bank(t)
                q = SPLIT_AT.get(t - 1)
                if q is not None and q not in POOL_LOW:
                    dve.wait_ge(xlo_set, q)
                    x_low(q, q % 2)
                if t - 1 in BIAS_PRODUCTS:
                    bias_sum(BIAS_PRODUCTS.index(t - 1) + 1)
            y_low(0, 0)
            mix_full(0)
            mix_low(0, 0)
            y_low(1, 1)
            dve.wait_ge(vcol_set, NL)
            finish(0, 0, 0, 1)
            mix_full(1)
            mix_low(1, 1)

            dve.wait_ge(xlo_set, 4)

            def step(q, it, par, it_prev):
                if not isinstance(q, int) or q + 1 < NQ:
                    x_low(q + 1, 1 - par)
                y_high(q - 1, it_prev, 1 - par)
                finish(q - 2, it - 1, par, 1)
                mix_full(q - 1)
                y_low(q - 1, 1 - par)
                mix_low(q - 1, 1 - par)

            step(3, 1, 1, 1)
            with dve.Fori(PEEL // 2, NQ // 2 - 1) as it:
                step(2 * it, it, 0, it - 1)
                step(2 * it + 1, it, 1, it)
            step(NQ - 2, NQ // 2 - 1, 0, NQ // 2 - 2)
            step(NQ - 1, NQ // 2 - 1, 1, NQ // 2 - 1)
            mix_full(NQ - 1)
            mix_low(NQ - 1, 1)
            finish(NQ - 2, NQ // 2 - 1, 0, 1)
            for h in range(2):
                dve.wait_ge(yhi_set, NQ + h)
                half = (slice(None), 1, slice(None), slice(2 * h, 2 * h + 2))
                nc.vector.tensor_tensor(y_lo[half], y_sb[half], y_hi[half].bitcast(F32),
                                        ALU.subtract).then_inc(ylo_set, 1)
            finish(NQ - 1, NQ // 2 - 1, 1, 1)
            finish(NQ - 1, NQ // 2 - 1, 1, 3)


def toeplitz(weight):
    w = weight.reshape(G, CG, CG, TAPS)
    out = np.zeros((CG, PH, 2, G, 2, CG, QP), weight.dtype)
    for p in range(PH):
        for n in range(PH):
            for d in range(2):
                tap = p + PH * d - n
                if 0 <= tap < TAPS:
                    out[:, p, d, :, n % 2, :, n // 2] = w[:, :, :, tap].transpose(2, 0, 1)
    return out.reshape(128, 2, G, 128)


def kernel(**inputs):
    import concourse.bacc as bacc
    from concourse.bass_utils import run_bass_kernel_spmd

    a = {k: np.asarray(v) for k, v in inputs.items()}
    f = np.float32
    mixes = [f"L{n}_cond_" for n in (1, 2, 3)]

    x = np.pad(a["x"], ((0, 0), (0, 0), (PAD, PH - PAD)))
    x = x.reshape(NQ, S, G, CG, JX, PH).transpose(0, 3, 5, 2, 1, 4).reshape(NQ * 128, G * S * JX)
    eye_tap = np.zeros((CG, PH, 2, 2, CG, QP), f)
    for c in range(CG):
        for n in range(PH):
            d, p = divmod(n + PAD, PH)
            eye_tap[c, p, d, n % 2, c, n // 2] = 1
    parity = np.zeros((G, 2, CG, 2), f)
    parity[:, 0, :, 0] = 1
    parity[:, 1, :, 1] = 1
    eye = np.eye(C, dtype=f)

    def table_rows(w, m_is_out):
        w = np.concatenate([w, eye[None]])
        w = w if m_is_out else w.transpose(0, 2, 1)
        return w.reshape(KR, C, 2, NH).transpose(0, 3, 2, 1)

    def pack(parts, widths):
        parts = [np.asarray(parts[n]).reshape(-1, w) for n, w in widths.items()]
        rows = max(len(p) for p in parts)
        return np.concatenate([np.pad(p, ((0, rows - len(p)), (0, 0))) for p in parts], 1)

    ws = [a[p + "weight"].reshape(K, C, C) for p in mixes]
    net = {
        "cond": a["cond_128"].T,
        "w0": np.stack([a[p + "W0"] for p in mixes], 1),
        "w1": np.stack([a[p + "W1"] for p in mixes], 1),
        "w2": np.stack([a[p + "W2"] for p in mixes], 1),
        "b01": np.stack([np.stack([a[p + b] for p in mixes], 1) for b in ("b0", "b1")], 1),
        "cw": a["L0_cond_c_weight"].T,
        "fcol": a["fside_S_0"],
    }
    biask = np.stack([a[p + "bias_k"].reshape(K * C) for p in mixes])
    arrays = {
        "x": x,
        "net": pack(net, NET),
        "kept": pack({"ident": np.eye(128, dtype=f), "parity": parity}, KEPT),
        "row": pack({"frow": a["fside_S_0"], "b2": np.concatenate([a[p + "b2"] for p in mixes])}, ROW),
        "toep": pack({"toep": toeplitz(a["L0_cond_weight"]), "eye_tap": eye_tap}, TOEP),
        "mixrow": np.concatenate([np.stack([w.transpose(2, 0, 1).reshape(C, K * C) for w in ws], 1),
                                  biask[None]]),
        "mats": np.stack([table_rows(w, n == 0) for n, w in enumerate(ws)], 1).reshape(KR * CH, CW),
    }
    nc = bacc.Bacc("TRN2", target_bir_lowering=False, num_devices=1)
    sent, args = {}, []
    for name, v in arrays.items():
        v = np.ascontiguousarray(v)
        sent[f"in_{name}"] = v
        args.append(nc.dram_tensor(f"in_{name}", v.shape, mybir.dt.from_np(v.dtype), kind="ExternalInput").ap())
    args.append(nc.dram_tensor("out", (NQ * 128, S * QP * J), F32, kind="ExternalOutput").ap())
    cond_resid_kernel(nc, *args)
    got = run_bass_kernel_spmd(nc, [sent], core_ids=[0]).results[0]["out"]
    return got.reshape(NQ, G, 2, CG, S, QP, J).transpose(0, 4, 1, 3, 6, 5, 2).reshape(B, C, L)
```
